# Optimizing a Trainium2 kernel written in Bass

```python
import numpy as np
import jax
import jax.numpy as jnp

def _softmax(x, axis=-1):
    return jax.nn.softmax(x, axis=axis)

def _gelu(x):
    return jax.nn.gelu(x, approximate=True)

def _silu(x):
    return jax.nn.silu(x)

def _sigmoid(x):
    return jax.nn.sigmoid(x)

def _layernorm(x, axis=-1, eps=1e-05):
    m = jnp.mean(x, axis=axis, keepdims=True)
    v = jnp.var(x, axis=axis, keepdims=True)
    return (x - m) / jnp.sqrt(v + eps)

def _scatter_add(tgt, idx, src, axis=0):
    return tgt.at[idx].add(src)

def _segment_sum(src, seg, n):
    return jax.ops.segment_sum(src, seg, n)
kernel_name = 'mk_gnn_preln_d4_gnn_r16_60fa2c'

def setup_inputs(seed: int=0):
    np.random.seed(seed)
    _w = jnp.asarray

    def _rec_inputs():
        import jax
        import jax.numpy as jnp
        _gk = jax.random.key(seed)
        x = -0.0007083 + 1.001 * jax.random.normal(jax.random.fold_in(_gk, 1), (6250, 16), jnp.float32)
        _s = jax.random.randint(jax.random.fold_in(_gk, 2), (100000,), 0, 6250, jnp.int32)
        _d = jax.random.randint(jax.random.fold_in(_gk, 3), (100000,), 0, 6250, jnp.int32)
        _loop = jnp.arange(6250, dtype=jnp.int32)
        src = jnp.concatenate([_s, _d, _loop])
        dst = jnp.concatenate([_d, _s, _loop])
        _o = jnp.argsort(dst, stable=True)
        src = src[_o]
        dst = dst[_o]
        edge_attr_16 = -3.57403e-05 + 0.999761 * jax.random.normal(jax.random.fold_in(_gk, 12), (206250, 16), jnp.float32)
        edge_attr_8 = -0.00010739 + 0.99994 * jax.random.normal(jax.random.fold_in(_gk, 13), (206250, 8), jnp.float32)
        edge_type_90 = jax.random.randint(jax.random.fold_in(_gk, 15), (206250,), 0, 90, jnp.int32)
        return (x, src, dst, edge_attr_16, edge_attr_8, edge_type_90)
    x, src, dst, edge_attr_16, edge_attr_8, edge_type_90 = _rec_inputs()

    def _L0_gnn_setup():
        import jax, jax.numpy as jnp
        import numpy as np
        N_NODES = 9375
        N_EDGES = 300000

        def gcn_conv(x, W, b, src, dst, n_nodes):
            h = x @ W
            ones = jnp.ones(dst.shape[0], dtype=h.dtype)
            deg = jax.ops.segment_sum(ones, dst, num_segments=n_nodes)
            dinv = jnp.where(deg > 0, jax.lax.rsqrt(deg), 0.0)
            norm = dinv[src] * dinv[dst]
            msgs = h[src] * norm[:, None]
            out = jax.ops.segment_sum(msgs, dst, num_segments=n_nodes)
            return out + b
        key = jax.random.key(seed)
        k1, k2, k3, k4 = jax.random.split(key, 4)
        x = jax.random.normal(k1, (N_NODES, 16), dtype=jnp.float32)
        edge_index = jax.random.randint(k2, (2, N_EDGES), 0, N_NODES, dtype=jnp.int64)
        W1 = jax.random.normal(k3, (16, 32), dtype=jnp.float32) * (1.0 / np.sqrt(16))
        b1 = jnp.zeros((32,), dtype=jnp.float32)
        W2 = jax.random.normal(k4, (32, 16), dtype=jnp.float32) * (1.0 / np.sqrt(32))
        b2 = jnp.zeros((16,), dtype=jnp.float32)
        return {'x': x, 'edge_index': edge_index, 'W1': W1, 'b1': b1, 'W2': W2, 'b2': b2}
    _L0_gnn_all = _L0_gnn_setup()
    _L0_gnn_in = {k: v for k, v in _L0_gnn_all.items() if k in ('W1', 'b1', 'W2', 'b2')}
    del _L0_gnn_all

    def _L1_gnn_setup():
        import jax, jax.numpy as jnp
        import numpy as np
        N_NODES = 1875
        N_EDGES = 18750
        IN_FEATS = 16
        OUT_FEATS = 16
        EDGE_DIM = 16
        key = jax.random.key(seed)
        ks = jax.random.split(key, 8)
        feat = jax.random.normal(ks[0], (N_NODES, IN_FEATS), dtype=jnp.float32)
        efeat = jax.random.normal(ks[1], (N_EDGES, EDGE_DIM), dtype=jnp.float32)
        W_msg = jax.random.normal(ks[2], (EDGE_DIM, IN_FEATS * OUT_FEATS), dtype=jnp.float32) * 0.1
        b_msg = jnp.zeros((IN_FEATS * OUT_FEATS,), dtype=jnp.float32)
        W_attn = jax.random.normal(ks[3], (EDGE_DIM, IN_FEATS * OUT_FEATS), dtype=jnp.float32) * 0.1
        b_attn = jnp.zeros((IN_FEATS * OUT_FEATS,), dtype=jnp.float32)
        src = jax.random.randint(ks[4], (N_EDGES,), 0, N_NODES, dtype=jnp.int32)
        dst = jax.random.randint(ks[5], (N_EDGES,), 0, N_NODES, dtype=jnp.int32)
        return {'feat': feat, 'efeat': efeat, 'W_msg': W_msg, 'b_msg': b_msg, 'W_attn': W_attn, 'b_attn': b_attn, 'src': src, 'dst': dst}
    _L1_gnn_all = _L1_gnn_setup()
    _L1_gnn_in = {k: v for k, v in _L1_gnn_all.items() if k in ('W_msg', 'b_msg', 'W_attn', 'b_attn')}
    del _L1_gnn_all

    def _L2_gnn_setup():
        import jax, jax.numpy as jnp
        import numpy as np
        N, E, IN, OUT, R, B = (3125, 50000, 16, 16, 90, 30)
        key = jax.random.key(seed)
        ks = jax.random.split(key, 9)
        h = jax.random.normal(ks[0], (N, IN), dtype=jnp.float32)
        he = jax.random.normal(ks[1], (E, IN), dtype=jnp.float32)
        Ws = jax.random.normal(ks[2], (OUT, IN), dtype=jnp.float32) * 0.1
        Wa = jax.random.normal(ks[3], (1, 3 * OUT), dtype=jnp.float32) * 0.1
        weight = jax.random.normal(ks[4], (B, IN, OUT), dtype=jnp.float32) * 0.1
        w_comp = jax.random.normal(ks[5], (R, B), dtype=jnp.float32) * 0.1
        src = jax.random.randint(ks[6], (E,), 0, N)
        dst = jax.random.randint(ks[7], (E,), 0, N)
        rel_type = jax.random.randint(ks[8], (E,), 0, R)
        return {'h': h, 'he': he, 'Ws': Ws, 'Wa': Wa, 'weight': weight, 'w_comp': w_comp, 'src': src, 'dst': dst, 'rel_type': rel_type}
    _L2_gnn_all = _L2_gnn_setup()
    _L2_gnn_in = {k: v for k, v in _L2_gnn_all.items() if k in ('Ws', 'Wa', 'weight', 'w_comp')}
    del _L2_gnn_all

    def _L3_gnn_setup():
        import jax, jax.numpy as jnp
        import numpy as np
        N_NODES = 6250
        N_EDGES = 100000
        IN_DIM = 16
        OUT_DIM = 16
        EDGE_DIM = 8
        key = jax.random.key(seed)
        ks = jax.random.split(key, 7)
        x = jax.random.normal(ks[0], (N_NODES, IN_DIM), dtype=jnp.float32)
        edge_attr = jax.random.normal(ks[1], (N_EDGES, EDGE_DIM), dtype=jnp.float32)
        root_w = jax.random.normal(ks[2], (IN_DIM, OUT_DIM), dtype=jnp.float32) * 0.1
        root_b = jax.random.normal(ks[3], (OUT_DIM,), dtype=jnp.float32) * 0.1
        edge_w = jax.random.normal(ks[4], (EDGE_DIM, OUT_DIM * IN_DIM), dtype=jnp.float32) * 0.1
        edge_b = jax.random.normal(ks[5], (OUT_DIM * IN_DIM,), dtype=jnp.float32) * 0.1
        edge_index = jax.random.randint(ks[6], (2, N_EDGES), 0, N_NODES, dtype=jnp.int64)
        return {'x': x, 'edge_attr': edge_attr, 'root_w': root_w, 'root_b': root_b, 'edge_w': edge_w, 'edge_b': edge_b, 'edge_index': edge_index}
    _L3_gnn_all = _L3_gnn_setup()
    _L3_gnn_in = {k: v for k, v in _L3_gnn_all.items() if k in ('root_w', 'root_b', 'edge_w', 'edge_b')}
    del _L3_gnn_all
    return {'x': x, 'src': src, 'dst': dst, 'edge_attr_16': edge_attr_16, 'edge_attr_8': edge_attr_8, 'edge_type_90': edge_type_90, 'L0_gnn_W1': _L0_gnn_in['W1'], 'L0_gnn_b1': _L0_gnn_in['b1'], 'L0_gnn_W2': _L0_gnn_in['W2'], 'L0_gnn_b2': _L0_gnn_in['b2'], 'L1_gnn_W_msg': _L1_gnn_in['W_msg'], 'L1_gnn_b_msg': _L1_gnn_in['b_msg'], 'L1_gnn_W_attn': _L1_gnn_in['W_attn'], 'L1_gnn_b_attn': _L1_gnn_in['b_attn'], 'L2_gnn_Ws': _L2_gnn_in['Ws'], 'L2_gnn_Wa': _L2_gnn_in['Wa'], 'L2_gnn_weight': _L2_gnn_in['weight'], 'L2_gnn_w_comp': _L2_gnn_in['w_comp'], 'L3_gnn_root_w': _L3_gnn_in['root_w'], 'L3_gnn_root_b': _L3_gnn_in['root_b'], 'L3_gnn_edge_w': _L3_gnn_in['edge_w'], 'L3_gnn_edge_b': _L3_gnn_in['edge_b']}

def reference(x, src, dst, edge_attr_16, edge_attr_8, edge_type_90, L0_gnn_W1, L0_gnn_b1, L0_gnn_W2, L0_gnn_b2, L1_gnn_W_msg, L1_gnn_b_msg, L1_gnn_W_attn, L1_gnn_b_attn, L2_gnn_Ws, L2_gnn_Wa, L2_gnn_weight, L2_gnn_w_comp, L3_gnn_root_w, L3_gnn_root_b, L3_gnn_edge_w, L3_gnn_edge_b):
    import jax
    import jax.numpy as jnp

    def _L0_gnn_ref(x, edge_index, W1, b1, W2, b2):
        import jax, jax.numpy as jnp
        import numpy as np
        N_NODES = 9375
        N_EDGES = 300000

        def gcn_conv(x, W, b, src, dst, n_nodes):
            h = x @ W
            ones = jnp.ones(dst.shape[0], dtype=h.dtype)
            deg = jax.ops.segment_sum(ones, dst, num_segments=n_nodes)
            dinv = jnp.where(deg > 0, jax.lax.rsqrt(deg), 0.0)
            norm = dinv[src] * dinv[dst]
            msgs = h[src] * norm[:, None]
            out = jax.ops.segment_sum(msgs, dst, num_segments=n_nodes)
            return out + b
        n = x.shape[0]
        loops = jnp.arange(n, dtype=edge_index.dtype)
        src = jnp.concatenate([edge_index[0], loops])
        dst = jnp.concatenate([edge_index[1], loops])
        h = jax.nn.relu(gcn_conv(x, W1, b1, src, dst, n))
        out = gcn_conv(h, W2, b2, src, dst, n)
        return out

    def _L1_gnn_ref(feat, efeat, W_msg, b_msg, W_attn, b_attn, src, dst):
        import jax, jax.numpy as jnp
        import numpy as np
        N_NODES = 1875
        N_EDGES = 18750
        IN_FEATS = 16
        OUT_FEATS = 16
        EDGE_DIM = 16
        N, in_f = feat.shape
        E = efeat.shape[0]
        w_m = (efeat @ W_msg + b_msg).reshape(E, in_f, -1)
        w_a = (efeat @ W_attn + b_attn).reshape(E, in_f, -1)
        h_src = feat[src][:, :, None]
        e1 = w_m * h_src
        e2 = w_a * h_src
        seg_max = jax.ops.segment_max(e2, dst, num_segments=N)
        ex = jnp.exp(e2 - seg_max[dst])
        denom = jax.ops.segment_sum(ex, dst, num_segments=N)
        attn = ex / denom[dst]
        ft = jax.ops.segment_sum(e1 * attn, dst, num_segments=N)
        return ft.sum(axis=1)

    def _L2_gnn_ref(h, he, Ws, Wa, weight, w_comp, src, dst, rel_type):
        import jax, jax.numpy as jnp
        import numpy as np
        N, E, IN, OUT, R, B = (3125, 50000, 16, 16, 90, 30)
        n_nodes, in_dim = h.shape
        num_bases, _, out_dim = weight.shape
        num_rels = w_comp.shape[0]
        V = weight.reshape(in_dim, num_bases, out_dim)
        W_rel = jnp.matmul(w_comp, V).reshape(num_rels, in_dim, out_dim)
        h_src = h[src]
        z_src = h_src @ Ws.T
        z_dst = h[dst] @ Ws.T
        z_e = he @ Ws.T
        e = jnp.concatenate([z_src, z_e, z_dst], axis=1) @ Wa.T
        msg = jnp.einsum('ei,eio->eo', h_src, W_rel[rel_type]) * e
        h_out = jax.ops.segment_sum(msg, dst, num_segments=n_nodes)
        return h_out

    def _L3_gnn_ref(x, edge_attr, root_w, root_b, edge_w, edge_b, edge_index):
        import jax, jax.numpy as jnp
        import numpy as np
        N_NODES = 6250
        N_EDGES = 100000
        IN_DIM = 16
        OUT_DIM = 16
        EDGE_DIM = 8
        src = edge_index[0]
        dst = edge_index[1]
        weights = (edge_attr @ edge_w + edge_b).reshape(-1, OUT_DIM, IN_DIM)
        msg = jnp.einsum('eoi,ei->eo', weights, x[src])
        out = x @ root_w + root_b
        out = out.at[dst].add(msg)
        return out
    edge_index = jnp.stack([src, dst])
    h = jnp.maximum(_layernorm(x, axis=-1), 0.0)
    x = x + _L0_gnn_ref(h, edge_index, L0_gnn_W1, L0_gnn_b1, L0_gnn_W2, L0_gnn_b2)
    h = jnp.maximum(_layernorm(x, axis=-1), 0.0)
    x = x + _L1_gnn_ref(h, edge_attr_16, L1_gnn_W_msg, L1_gnn_b_msg, L1_gnn_W_attn, L1_gnn_b_attn, src, dst)
    h = jnp.maximum(_layernorm(x, axis=-1), 0.0)
    x = x + _L2_gnn_ref(h, edge_attr_16, L2_gnn_Ws, L2_gnn_Wa, L2_gnn_weight, L2_gnn_w_comp, src, dst, edge_type_90)
    h = jnp.maximum(_layernorm(x, axis=-1), 0.0)
    x = x + _L3_gnn_ref(h, edge_attr_8, L3_gnn_root_w, L3_gnn_root_b, L3_gnn_edge_w, L3_gnn_edge_b, edge_index)
    return x

_drawn_inputs = setup_inputs


def setup_inputs(seed=0):
    import zlib

    import numpy as np

    out = dict(_drawn_inputs(seed))
    spreads = {'L0_gnn_b1': (0.0, 0.1),
     'L0_gnn_b2': (0.0, 0.1),
     'L1_gnn_b_msg': (0.0, 0.1),
     'L1_gnn_b_attn': (0.0, 0.34)}
    factors = {'L3_gnn_root_b': 4.061}
    for name, (base, spread) in spreads.items():
        noise = np.random.default_rng([zlib.crc32(name.encode()), seed]).standard_normal(out[name].shape)
        drawn = base * np.exp(spread * noise) if base else spread * noise
        out[name] = jnp.asarray(drawn.astype(out[name].dtype))
    for name, factor in factors.items():
        out[name] = (out[name] * factor).astype(out[name].dtype)
    return out
```

```python
import concourse.bass as bass
from concourse import mybir
from contextlib import ExitStack

N, E, F = 6250, 206250, 16
P = 125
C = E // P
J = N // P
R = 90
NB = 30
D8 = 8
BL = 50
NBL = C // BL
HALF = (NBL - 1) // 2
B1 = 10
NB1 = C // B1
HALF1 = (NB1 - 1) // 2
SUB = 33
SUBW = C // SUB
CH = F * F
ROW = 3 * CH
KX = 6 * F + 3
TW = F + 1
PW = F * D8 + F
BIG = 1e38
FAR = 1.0e6
EPS = 1e-5
NARROW = ("conv1", "conv2", "rel", "nn")
WIDTH = {"conv1": F, "conv2": F, "rel": 2 * F, "nn": F}
GROW = {"conv1": F, "conv2": F, "rel": TW, "nn": PW}


def graph_layers(nc, A, out):
    f32, i32, bf16 = mybir.dt.float32, mybir.dt.int32, mybir.dt.bfloat16
    ALU, ACT, AX = mybir.AluOpType, mybir.ActivationFunctionType, mybir.AxisListType
    X = AX.X

    ctx = ExitStack()
    with ctx:
        def sb(name, shape, dt=f32):
            return ctx.enter_context(nc.sbuf_tensor(name, shape, dt))

        def dram(name, shape, dt=f32):
            return nc.dram_tensor(name, shape, dt).ap()

        sems = {}

        def S(name):
            if name not in sems:
                sems[name] = ctx.enter_context(nc.semaphore(name))
            return sems[name]

        total = {"i0": 16 * (HALF + 1), "i1": 16 * HALF, "g0": 16 * BL * (HALF + 1), "g1": 16 * BL * HALF,
                 "r0": 16 * (HALF + 1), "r1": 16 * HALF, "used": NBL, "run": NBL, "hg": 16, "hs": 16,
                 "ns": 16 * J, "merged": 1, "tt": 1, "cs": 1, "cb": 1}

        def upto(L, key, value):
            return value + NARROW.index(L) * total[key]

        x = sb("x", [P, J, F])
        h = sb("h", [P, J, F])
        tmp = sb("tmp", [P, J, F])
        tmp2 = sb("tmp2", [P, J, F])
        st1 = sb("st1", [P, J])
        st2 = sb("st2", [P, J])
        keep = sb("keep", [P, C])
        gate_e = sb("gate_e", [P, C])
        dinv = sb("dinv", [P, J])
        has = sb("has", [P, J])
        ncol = sb("ncol", [P, J])
        rp = sb("rp", [P, J])
        rpn = sb("rpn", [P, J])
        qf = sb("qf", [P, J])
        endpos = sb("endpos", [P, J], i32)
        qi = sb("qi", [P, J], i32)
        si = sb("si", [P, J], i32)
        first_dst = sb("first_dst", [P, 1], i32)
        head_pos = sb("head_pos", [P, 1], i32)
        head_row = sb("head_row", [P, 1], i32)
        head_node = sb("head_node", [P, 1], i32)
        hv = sb("hv", [P, 4])
        one_run = sb("one_run", [P, 1])
        ident = sb("ident", [128, 128])
        identb = sb("identb", [128, 128], bf16)
        ones = sb("ones", [128, 128])
        diag = sb("diag", [P, P])
        runT = sb("runT", [128, P])
        resT = sb("resT", [128, P])
        nodeT = sb("nodeT", [F, J * P])
        small = sb("small", [128, 1060])
        wk = sb("wk", [F, R * TW])
        w1 = sb("w1", [F, 2 * F])
        w2 = sb("w2", [2 * F, F])
        bias = sb("bias", [P, 3, F])
        b1c = sb("b1c", [2 * F, 1])
        gdst = sb("gdst", [P, F])
        src_slot = sb("src_slot", [P, 2, BL], i32)
        carryT = sb("carryT", [128, 128])
        headb = sb("headb", [P, 2 * F])
        poolw = sb("poolw", [1, 2])
        arena = sb("arena", [128, 35600])

        def ar(a, n):
            return arena[0:P, a:a + n]

        G = ar(0, 2 * BL * PW)
        o = 2 * BL * PW
        V = ar(o, BL * 2 * F); o += BL * 2 * F
        TM = ar(o, BL * F * D8); o += BL * F * D8
        SR = ar(o, 2 * BL * 2 * F); o += 2 * BL * 2 * F
        EA = ar(o, 2 * BL * F); o += 2 * BL * F
        assert o <= 35600
        X6 = ar(4 * BL * F, BL * 50).bitcast(bf16).rearrange("p (c k) -> p c k", k=100)
        r1 = ar(TM_AT := 2 * BL * PW + BL * 2 * F, BL * F).rearrange("p (c f) -> p c f", f=F)
        r2 = ar(TM_AT + BL * F, BL * F).rearrange("p (c f) -> p c f", f=F)
        X6T = arena[0:KX, 6000:6000 + 2 * B1 * P // 2].bitcast(bf16).rearrange("p (s c) -> p s c", s=2)
        o = 0
        XS = ar(o, 2 * B1 * ROW).rearrange("p (s t c) -> p s t c", s=2, t=B1); o += 2 * B1 * ROW
        EE = ar(o, B1 * 2 * CH).rearrange("p (t i c) -> p t i c", t=B1, i=F); o += B1 * 2 * CH
        GH = ar(o, 2 * B1 * F).rearrange("p (s t f) -> p s t f", s=2, t=B1); o += 2 * B1 * F
        XT = arena[0:KX, o:o + 2 * B1 * P // 2].bitcast(bf16).rearrange("p (s c) -> p s c", s=2); o += B1 * P
        W6 = arena[0:KX, o:o + CH].bitcast(bf16); o += CH
        KR = ar(o, 2 * 2 * B1).rearrange("p (s t k) -> p s t k", s=2, k=2); o += 4 * B1
        END = ar(o, 2 * B1).bitcast(i32).rearrange("p (s t) -> p s t", s=2); o += 2 * B1
        SRC1 = ar(o, 2 * B1).bitcast(i32).rearrange("p (s t) -> p s t", s=2); o += 2 * B1
        DC = ar(o, CH); o += CH
        SC = ar(o, 2 * CH).rearrange("p (a c) -> p a c", a=2); o += 2 * CH
        CT = arena[:, o:o + 6 * P].rearrange("p (a c) -> p a c", a=6); o += 6 * P
        YT = arena[:, o:o + 6 * 126].rearrange("p (a c) -> p a c", a=6); o += 6 * 126
        FT = arena[:, o:o + 4 * P].rearrange("p (a c) -> p a c", a=4); o += 4 * P
        CB = ar(o, ROW); o += ROW
        HG = ar(o, ROW); o += ROW
        HM = ar(o, 3 * CH).rearrange("p (a c) -> p a c", a=3); o += 3 * CH
        W1F = arena[0:F + 1, o:o + 2 * CH]; o += 2 * CH
        W1R = arena[0:F + 1, o:o + 2 * CH]; o += 2 * CH
        W1B = arena[0:F + 1, o:o + 3 * CH].bitcast(bf16).rearrange("p (a c) -> p a c", a=3); o += 3 * CH
        assert o <= 35600, o
        NODE = ar(0, 2 * 5 * ROW).rearrange("p (s j c) -> p s j c", s=2, j=5)
        o = 0
        dsti = ar(o, C).bitcast(i32); o += C
        prevd = ar(o, C).bitcast(i32); o += C
        nextd = ar(o, C).bitcast(i32); o += C
        srci = ar(o, C).bitcast(i32); o += C
        typi = ar(o, C).bitcast(i32); o += C
        wide = ar(o, J * P); o += J * P
        g2 = ar(o, J * SUB).bitcast(i32); o += J * SUB
        g3 = ar(o, J * SUBW).bitcast(i32); o += J * SUBW
        KR0 = ar(o, 2 * C).rearrange("p (c k) -> p c k", k=2); o += 2 * C
        fend = ar(o, C); o += C
        iend = ar(o, C).bitcast(i32); o += C
        irel = ar(o, C).bitcast(i32); o += C
        subi = ar(o, SUB).bitcast(i32); o += SUB
        zero = ar(o, 3840); o += 3840
        assert o <= 35600, o
        TR = arena[0:P, 0:4 * R * TW].rearrange("p (s c) -> p s c", s=4)
        TP = arena[0:P, 0:J * (PW + F)].rearrange("p (j c) -> p j c", j=J)
        HT32 = arena[0:2 * F, 0:J * P]
        NS = ar(20000, J * 2 * F)

        PS = ctx.enter_context(nc.psum_tensor("PS", [128, 4096], f32))

        d_h = dram("d_h", [N, F])
        d_sub = dram("d_sub", [P, SUB], i32)
        d_rp = dram("d_rp", [N + 1, 1])
        d_end = dram("d_end", [N, 1], i32)
        d_kr = dram("d_kr", [E, 2])
        d_iend = dram("d_iend", [E], i32)
        d_irel = dram("d_irel", [E], i32)
        d_x6 = dram("d_x6", [KX, C * P], bf16)
        d_w = dram("d_w", [F, R, F])
        d_soft = dram("d_soft", [N, ROW])
        d_rel = dram("d_rel", [N * R, TW])
        d_nn = dram("d_nn", [N, PW])
        d_run = {k: dram(f"d_run_{k}", [E, WIDTH[k]]) for k in NARROW}
        d_tab = {"conv1": d_h, "conv2": dram("d_h2", [N, F]), "rel": d_rel, "nn": d_nn}
        d_feat = dram("d_feat", [N, F])
        d_index = {"conv1": A["src"], "conv2": A["src"], "rel": d_irel, "nn": A["src"]}

        def nodes(t):
            return t.rearrange("(p j) f -> p (j f)", p=P)

        def edges(t):
            return t.rearrange("(p c) -> p c", p=P)

        def edges_w(t):
            return t.rearrange("(p c) f -> p (c f)", p=P)

        def flat(t):
            return t.rearrange("p j f -> p (j f)")

        ea16 = edges_w(A["edge_attr_16"])
        ea8 = edges_w(A["edge_attr_8"])

        def blocks(step, half, fori):
            step(0, 0, 0, True)
            step(1, 1, 0, True)
            with fori(1, half) as k:
                step(2 * k, 0, k, False)
                step(2 * k + 1, 1, k, False)
            step(2 * half, 0, half, False)

        block = ctx.enter_context(nc.Block())

        @block.sync
        def _(sp):
            dst = A["dst"]
            sp.dma_start(dsti, edges(dst)).then_inc(S("l_dst"), 16)
            sp.wait_ge(S("cst"), 1)
            sp.dma_start(prevd[0:1, 1:C], dst[0:C - 1].rearrange("(a c) -> a c", a=1)).then_inc(S("l_nb"), 16)
            sp.dma_start(prevd[1:P, :], dst[C - 1:E - 1].rearrange("(p c) -> p c", c=C)).then_inc(S("l_nb"), 16)
            sp.dma_start(nextd[0:P - 1, :], dst[1:E - C + 1].rearrange("(p c) -> p c", c=C)).then_inc(S("l_nb"), 16)
            sp.dma_start(nextd[P - 1:P, 0:C - 1], dst[E - C + 1:E].rearrange("(a c) -> a c", a=1)).then_inc(S("l_nb"), 16)
            sp.dma_start(flat(x), nodes(A["x"])).then_inc(S("l_x"), 16)
            sp.dma_start(srci, edges(A["src"])).then_inc(S("l_st"), 16)
            sp.dma_start(typi, edges(A["edge_type_90"])).then_inc(S("l_st"), 16)
            sp.dma_start(w1[:, :], A["L0_gnn_W1"]).then_inc(S("l_w"), 16)
            sp.dma_start(w2[:, :], A["L0_gnn_W2"]).then_inc(S("l_w"), 16)
            sp.dma_start(b1c[:, :], A["L0_gnn_b1"].rearrange("(f a) -> f a", a=1)).then_inc(S("l_w"), 16)
            for n, b in enumerate(("L0_gnn_b2", "L3_gnn_root_b")):
                sp.dma_start(bias[:, n, :], A[b].partition_broadcast(P)).then_inc(S("l_w"), 16)
            sp.dma_start(small[0:F, 0:F], A["L2_gnn_Ws"]).then_inc(S("l_w"), 16)
            for n in range(3):
                sp.dma_start(small[0:F, 16 + n:17 + n],
                             A["L2_gnn_Wa"][0, n * F:(n + 1) * F].rearrange("(o a) -> o a", a=1)).then_inc(S("l_w"), 16)
            sp.dma_start(small[0:R, 32:32 + NB], A["L2_gnn_w_comp"]).then_inc(S("l_w"), 16)
            sp.dma_start(small[0:NB, 64:64 + F * F].rearrange("b (a o) -> b a o", a=F),
                         A["L2_gnn_weight"].rearrange("b i o -> (b i o)")
                         .rearrange("(a b o) -> b a o", a=F, b=NB)).then_inc(S("l_w"), 16)
            sp.wait_ge(S("sub"), 1)
            sp.dma_start(d_sub, subi).then_inc(S("d_sub"), 16)
            sp.wait_ge(S("d_sub"), 16)
            sp.dma_start(small[0:1, 400:400 + P].bitcast(i32), d_sub[:, 0:1].rearrange("p a -> a p"),
                         allow_slow_non_contiguous=True).then_inc(S("l_bnd"), 16)
            sp.wait_ge(S("zero"), 1)
            for n in range(10):
                sp.dma_start(nodes(d_soft)[:, n * 3840:(n + 1) * 3840], zero).then_inc(S("d_zero"), 16)
            sp.wait_ge(S("krs"), 1)
            sp.dma_start(edges_w(d_kr), KR0.rearrange("p c k -> p (c k)")).then_inc(S("d_idx"), 16)
            sp.dma_start(edges(d_iend), iend).then_inc(S("d_idx"), 16)
            sp.dma_start(edges(d_irel), irel).then_inc(S("d_idx"), 16)
            sp.wait_ge(S("rp"), 1)
            sp.dma_start(nodes(d_rp[0:N, :]), rp[:, :]).then_inc(S("d_rp"), 16)
            sp.dma_start(d_rp[N:N + 1, :], hv[0:1, 3:4]).then_inc(S("d_rp"), 16)
            sp.wait_ge(S("d_rp"), 32)
            sp.dma_start(rpn[:, :], nodes(d_rp[1:N + 1, :])).then_inc(S("l_rpn"), 16)
            sp.wait_ge(S("endpos"), 1)
            sp.dma_start(nodes(d_end), endpos[:, :]).then_inc(S("d_end"), 16)
            sp.wait_ge(S("h_conv1"), 1)
            sp.dma_start(nodes(d_h), flat(h)).then_inc(S("tab_conv1"), 16)
            sp.wait_ge(S("d_idx"), 48)
            sp.wait_ge(S("d_zero"), 160)

            def narrow(L):
                index = edges(d_index[L])

                def step(b, s, k, first):
                    if not first:
                        sp.wait_ge(S(f"n_g{s}"), upto(L, f"g{s}", 16 * BL * k))
                    sp.dma_start(src_slot[:, s, :], index[:, bass.ds(b * BL, BL)]).then_inc(S(f"n_i{s}"), 16)
                    if L == "conv1":
                        if not first:
                            sp.wait_ge(S("split"), b - 1)
                        sp.dma_start(EA[:, s * BL * F:(s + 1) * BL * F],
                                     ea16[:, bass.ds(b * (BL * F), BL * F)]).then_inc(S(f"ea16_{s}"), 16)
                    if L == "nn":
                        if not first:
                            sp.wait_ge(S("n_used"), upto(L, "used", b - 1))
                        sp.dma_start(EA[:, s * BL * D8:(s + 1) * BL * D8],
                                     ea8[:, bass.ds(b * (BL * D8), BL * D8)]).then_inc(S(f"ea8_{s}"), 16)

                blocks(step, HALF, sp.Fori)

            narrow("conv1")
            sp.wait_ge(S("h_conv2"), 1)
            sp.dma_start(nodes(d_tab["conv2"]), flat(h)).then_inc(S("tab_conv2"), 16)
            sp.wait_ge(S("n_g0"), 16 * BL * (HALF + 1))
            sp.wait_ge(S("n_g1"), 16 * BL * HALF)
            narrow("conv2")
            sp.wait_ge(S("conv2_nodes"), 1)
            for n, k in enumerate(("attn", "msg")):
                w = W1F.rearrange("p (i a o) -> p i a o", i=F, a=2)[:, :, n, :]
                sp.dma_start(w[0:F], A[f"L1_gnn_W_{k}"].rearrange("k (i o) -> k i o", i=F)).then_inc(S("l_w1"), 16)
                sp.dma_start(w[F:F + 1], A[f"L1_gnn_b_{k}"].rearrange("(a i o) -> a i o", a=1, i=F)).then_inc(S("l_w1"), 16)
            sp.wait_ge(S("w1_parts"), 3)
            for n, part in enumerate((0, 1, 2, 0, 1, 0)):
                sp.dma_start(W6[n * F:(n + 1) * F, :], W1B[0:F, part, :]).then_inc(S("l_w6"), 16)
            for part in range(3):
                sp.dma_start(W6[6 * F + part:6 * F + part + 1, :], W1B[F:F + 1, part, :]).then_inc(S("l_w6"), 16)
            sp.wait_ge(S("h_soft"), 1)
            sp.dma_start(nodes(d_feat), flat(h)).then_inc(S("tab_soft"), 16)
            sp.wait_ge(S("x6_0"), 16 * (5 * HALF + 3))
            sp.wait_ge(S("x6_1"), 16 * (5 * HALF + 2))

            def soft(b, s, k, first):
                if not first:
                    sp.wait_ge(S(f"soft_g{s}"), 16 * B1 * k)
                sp.dma_start(SRC1[:, s, :], edges(A["src"])[:, bass.ds(b * B1, B1)]).then_inc(S(f"soft_i{s}"), 16)
                if not first:
                    sp.wait_ge(S("soft_done"), b - 1)
                sp.dma_start(KR[:, s], edges_w(d_kr)[:, bass.ds(b * (2 * B1), 2 * B1)].rearrange("p (t k) -> p t k", k=2))\
                    .then_inc(S(f"soft_k{s}"), 16)
                sp.dma_start(XT[:, s, :], d_x6[:, bass.ds(b * (B1 * P), B1 * P)]).then_inc(S(f"soft_x{s}"), 16)
                if not first:
                    sp.wait_ge(S(f"soft_s{s}"), 16 * B1 * k)
                sp.dma_start(END[:, s, :], edges(d_iend)[:, bass.ds(b * B1, B1)]).then_inc(S(f"soft_e{s}"), 16)

            blocks(soft, HALF1, sp.Fori)
            sp.wait_ge(S("soft_heads"), 16)
            for n in range(J // 5):
                if n >= 2:
                    sp.wait_ge(S("soft_n"), n - 1)
                sp.dma_start(NODE[:, n % 2].rearrange("p j c -> p (j c)"),
                             nodes(d_soft)[:, n * 5 * ROW:(n + 1) * 5 * ROW]).then_inc(S(f"soft_l{n % 2}"), 16)
            sp.wait_ge(S("wrel"), 1)
            sp.dma_start(d_w.rearrange("a r o -> r a o"), small[0:R, 640:896].rearrange("r (a o) -> r a o", a=F))\
                .then_inc(S("d_w"), 16)
            sp.wait_ge(S("d_w"), 16)
            sp.dma_start(wk[:, :].rearrange("i (r c) -> i r c", c=TW)[:, :, 0:F],
                         d_w.rearrange("a r o -> (a r o)").rearrange("(r i o) -> i r o", i=F, o=F)).then_inc(S("l_wk"), 16)
            for j in range(J):
                sp.wait_ge(S("rel_act"), 2 * (j + 1))
                sp.wait_ge(S("rel_evd"), j + 1)
                sp.dma_start(d_rel.rearrange("(p j r) c -> p j (r c)", p=P, j=J)[:, j, :], TR[:, j % 4, :])\
                    .then_inc(S(f"rel_t{j % 4}"), 16)
            for s in range(4):
                sp.wait_ge(S(f"rel_t{s}"), 16 * ((J - s + 3) // 4))
            narrow("rel")
            sp.wait_ge(S("rel_nodes"), 1)
            for k in range(D8):
                sp.dma_start(wk[:, 0:F * D8].rearrange("i (o k) -> i o k", k=D8)[:, :, k:k + 1],
                             A["L3_gnn_edge_w"][k, :].rearrange("(o i) -> i o", i=F).unsqueeze(2), allow_slow_non_contiguous=True).then_inc(S("l_w3"), 16)
            sp.dma_start(wk[:, F * D8:PW].unsqueeze(2), A["L3_gnn_edge_b"].rearrange("(o i) -> i o", i=F).unsqueeze(2), allow_slow_non_contiguous=True).then_inc(S("l_w3"), 16)
            sp.dma_start(wk[:, PW:PW + F], A["L3_gnn_root_w"]).then_inc(S("l_w3"), 16)
            sp.wait_ge(S("nn_rows"), 1)
            sp.dma_start(d_nn.rearrange("(p j) c -> p j c", p=P), TP[:, :, 0:PW]).then_inc(S("tab_nn"), 16)
            sp.wait_ge(S("tab_nn"), 16)
            narrow("nn")
            sp.wait_ge(S("x_out"), 1)
            sp.dma_start(nodes(out), flat(x)).then_inc(S("out"), 16)
            sp.wait_ge(S("out"), 16)

        @block.gpsimd
        def _(gp):
            gp.memset(prevd[0:1, 0:1], -1)
            gp.memset(zero, 0.0).then_inc(S("zero"), 1)
            gp.memset(poolw[:, :], 0.0).then_inc(S("pw"), 1)
            gp.iota(qi[:, :], pattern=[[1, J]], base=0, channel_multiplier=J).then_inc(S("iota"), 1)
            gp.memset(ident[:, :], 0.0).then_inc(S("id"), 1)
            gp.wait_ge(S("id"), 1)
            gp.affine_select(out=ident[:, :], in_=ident[:, :], compare_op=ALU.not_equal, fill=1.0,
                             base=0, pattern=[[-1, 128]], channel_multiplier=1).then_inc(S("id"), 1)
            gp.iota(small[0:P, 600:601].bitcast(i32), pattern=[[1, 1]], base=C, channel_multiplier=C).then_inc(S("iota"), 1)

            def gather(dst, table, index, sem):
                gp.indirect_dma_start(out=dst, out_offset=None, in_=table,
                                      in_offset=bass.IndirectOffsetOnAxis(ap=index, axis=0)).then_inc(S(sem), 16)

            def scatter(table, index, src, sem):
                gp.indirect_dma_start(out=table, out_offset=bass.IndirectOffsetOnAxis(ap=index, axis=0), in_=src,
                                      in_offset=None, bounds_check=table.shape[0] - 1, oob_is_err=False).then_inc(S(sem), 16)

            tick = [1]

            def hold(value):
                gp.wait_ge(S("pw"), value)
                gp.tensor_tensor(poolw[:, 0:1], poolw[:, 1:2], poolw[:, 1:2], ALU.add).then_inc(S("pw"), 1)

            gp.wait_ge(S("q1"), 1)
            gp.wait_ge(S("d_sub"), 16)
            for j in range(J):
                gather(g2[:, j * SUB:(j + 1) * SUB], d_sub, qi[:, j:j + 1], "g_sub")
            gp.wait_ge(S("q2"), 1)
            rows = A["dst"].rearrange("(r w) -> r w", w=SUBW)
            for j in range(J):
                gather(g3[:, j * SUBW:(j + 1) * SUBW], rows, si[:, j:j + 1], "g_row")
            gp.wait_ge(S("d_end"), 16)
            gp.wait_ge(S("l_fd"), 16)
            gather(head_pos[:, :], d_end, first_dst[:, :], "g_head")

            def narrow(L):
                W = GROW[L]
                g = G[:, 0:2 * BL * W].rearrange("p (s t w) -> p s t w", s=2, t=BL)
                base = tick[0]

                def step(b, s, k, first):
                    gp.wait_ge(S(f"n_i{s}"), upto(L, f"i{s}", 16 * (k + 1)))
                    if not first:
                        gp.wait_ge(S("n_used"), upto(L, "used", b - 1))
                    hold(b + base)
                    for t in range(BL):
                        gather(g[:, s, t, :], d_tab[L], src_slot[:, s, t:t + 1], f"n_g{s}")

                blocks(step, HALF, gp.Fori)
                tick[0] += NBL
                w = WIDTH[L]
                gp.wait_ge(S("n_r0"), upto(L, "r0", 16 * (HALF + 1)))
                gp.wait_ge(S("n_r1"), upto(L, "r1", 16 * HALF))
                gather(headb[:, 0:w], d_run[L], head_pos[:, :], "n_hg")
                gp.wait_ge(S("n_merged"), upto(L, "merged", 1))
                scatter(d_run[L], head_row[:, :], headb[:, 0:w], "n_hs")
                gp.wait_ge(S("n_hs"), upto(L, "hs", 16))
                for j in range(J):
                    gather(NS[:, j * w:(j + 1) * w], d_run[L], endpos[:, j:j + 1], "n_ns")

            gp.wait_ge(S("tab_conv1"), 16)
            gp.wait_ge(S("d_idx"), 48)
            gp.wait_ge(S("d_zero"), 160)
            narrow("conv1")
            gp.wait_ge(S("tab_conv2"), 16)
            narrow("conv2")

            base = tick[0]

            def soft_gather(b, s, k, first):
                gp.wait_ge(S(f"soft_i{s}"), 16 * (k + 1))
                if not first:
                    gp.wait_ge(S("soft_used"), b - 1)
                hold(b + base)
                for t in range(B1):
                    gather(GH[:, s, t, :], d_feat, SRC1[:, s, t:t + 1], f"soft_g{s}")

            sbase = base + NB1

            def soft_scatter(b, s, k):
                gp.wait_ge(S(f"soft_e{s}"), 16 * (k + 1))
                gp.wait_ge(S("soft_done"), b + 1)
                gp.wait_ge(S("sw"), b)
                gp.tensor_tensor(poolw[:, 0:1], poolw[:, 1:2], poolw[:, 1:2], ALU.add).then_inc(S("sw"), 1)
                for t in range(B1):
                    scatter(d_soft, END[:, s, t:t + 1], XS[:, s, t, :], f"soft_s{s}")

            gp.wait_ge(S("tab_soft"), 16)
            gp.wait_ge(S("conv2_nodes"), 1)
            gp.wait_ge(S("d_zero"), 160)

            def one(b, s, k):
                gp.wait_ge(S(f"soft_i{s}"), 16 * (k + 1))
                gp.wait_ge(S("soft_used"), b - 1)
                hold(2 * b + base - 1)
                for t in range(B1):
                    gather(GH[:, s, t, :], d_feat, SRC1[:, s, t:t + 1], f"soft_g{s}")

            def two(b, s, k, held):
                gp.wait_ge(S(f"soft_e{s}"), 16 * (k + 1))
                gp.wait_ge(S("soft_done"), b + 1)
                hold(held)
                for t in range(B1):
                    scatter(d_soft, END[:, s, t:t + 1], XS[:, s, t, :], f"soft_s{s}")

            for b in range(2):
                gp.wait_ge(S(f"soft_i{b}"), 16)
                hold(base + b)
                for t in range(B1):
                    gather(GH[:, b, t, :], d_feat, SRC1[:, b, t:t + 1], f"soft_g{b}")
            with gp.Fori(0, HALF1 - 1) as k:
                two(2 * k, 0, k, 4 * k + (base + 2))
                one(2 * k + 2, 0, k + 1)
                two(2 * k + 1, 1, k, 4 * k + (base + 4))
                one(2 * k + 3, 1, k + 1)
            b = 2 * HALF1 - 2
            two(b, 0, HALF1 - 1, 2 * b + base + 2)
            one(b + 2, 0, HALF1)
            two(b + 1, 1, HALF1 - 1, 2 * b + base + 4)
            two(b + 2, 0, HALF1, 2 * b + base + 5)
            tick[0] += 2 * NB1
            gp.wait_ge(S("soft_s0"), 16 * B1 * (HALF1 + 1))
            gp.wait_ge(S("soft_s1"), 16 * B1 * HALF1)
            gather(HG, d_soft, first_dst[:, :], "soft_hg")
            gp.wait_ge(S("soft_merged"), 1)
            scatter(d_soft, head_node[:, :], HG, "soft_heads")

            for s in range(4):
                gp.wait_ge(S(f"rel_t{s}"), 16 * ((J - s + 3) // 4))
            narrow("rel")
            gp.wait_ge(S("tab_nn"), 16)
            narrow("nn")

        @block.scalar
        def _(act):
            def store_runs(L):
                w = WIDTH[L]
                run = edges_w(d_run[L])
                return lambda b, s: act.dma_start(run[:, bass.ds(b * (BL * w), BL * w)],
                                                  SR[:, s * BL * w:(s + 1) * BL * w]).then_inc(S(f"n_r{s}"), 16)

            act.wait_ge(S("l_dst"), 16)
            act.dma_start(first_dst[:, :], edges(A["dst"])[:, 0:1], allow_slow_non_contiguous=True).then_inc(S("l_fd"), 16)

            def root(name):
                act.wait_ge(S(f"{name}_var"), 1)
                act.activation(st2[:, :], st1[:, :], ACT.Sqrt).then_inc(S(f"{name}_std"), 1)

            root("deg")
            root("ln1")

            def narrow(L):
                store = store_runs(L)

                def step(b, s, k, first):
                    act.wait_ge(S("n_run"), upto(L, "run", b + 1))
                    store(b, s)
                    if L == "conv1":
                        for g in range(5):
                            i = 5 * s + g
                            act.wait_ge(S("x6_tr"), 5 * b + g + 1)
                            if not first or i >= 2:
                                act.wait_ge(S(f"x6_{i % 2}"), 80 * k + 16 * (i // 2))
                            bank = PS[0:KX, (i % 2) * 1024:(i % 2) * 1024 + B1 * 64].bitcast(bf16)\
                                .rearrange("p (t c) -> p t c", t=B1)
                            act.activation(X6T[:, i % 2, :].rearrange("p (t c) -> p t c", t=B1), bank[:, :, 0:P],
                                           ACT.Copy).then_inc(S("x6_ev"), 1)
                            act.wait_ge(S("x6_ev"), 5 * b + g + 1)
                            act.dma_start(d_x6[:, bass.ds(b * (BL * P) + g * (B1 * P), B1 * P)], X6T[:, i % 2, :])\
                                .then_inc(S(f"x6_{i % 2}"), 16)

                blocks(step, HALF, act.Fori)

            narrow("conv1")
            act.wait_ge(S("x6_0"), 16 * (5 * HALF + 3))
            act.wait_ge(S("x6_1"), 16 * (5 * HALF + 2))
            for n in range((J + 3) // 4):
                act.wait_ge(S("t1"), n + 1)
                w = min(4, J - 4 * n) * P
                act.activation(nodeT[:, n * 500:n * 500 + w], PS[0:F, (n % 2) * 512:(n % 2) * 512 + w],
                               ACT.Copy).then_inc(S("t1_ev"), 1)
            act.wait_ge(S("l_w"), 16 * 10)
            for n in range((J + 3) // 4):
                act.wait_ge(S("hid"), n + 1)
                w = min(4, J - 4 * n) * P
                act.activation(HT32[:, n * 500:n * 500 + w], PS[0:2 * F, 1024 + (n % 2) * 512:1024 + (n % 2) * 512 + w],
                               ACT.Relu, bias=b1c[:, 0:1]).then_inc(S("hid_ev"), 1)
            narrow("conv2")
            root("ln2")

            def soft(b, s, k, first):
                for part in range(2):
                    act.wait_ge(S("soft_d"), 2 * b + part + 1)
                    half = XS[:, s, 5 * part:5 * part + 5, CH:2 * CH]
                    act.activation(half, half, ACT.Exp).then_inc(S("soft_exp"), 1)
                act.activation(DC, DC, ACT.Exp).then_inc(S("soft_exp"), 1)

            blocks(soft, HALF1, act.Fori)
            act.wait_ge(S("cd"), 2)
            act.activation(FT[:, :, :], FT[:, :, :], ACT.Exp).then_inc(S("ce"), 1)
            act.wait_ge(S("hd"), 1)
            act.activation(HM[:, 0:2, :], HM[:, 0:2, :], ACT.Exp).then_inc(S("he"), 1)
            root("ln3")
            for n in range((J + 3) // 4):
                act.wait_ge(S("t2"), n + 1)
                w = min(4, J - 4 * n) * P
                act.activation(nodeT[:, n * 500:n * 500 + w], PS[0:F, (n % 2) * 512:(n % 2) * 512 + w],
                               ACT.Copy).then_inc(S("t2_ev"), 1)
            for j in range(J):
                for n in range(2):
                    act.wait_ge(S("rel_mm"), 3 * j + n + 1)
                    if j >= 4:
                        act.wait_ge(S(f"rel_t{j % 4}"), 16 * (j // 4))
                    bank = 1024 + ((3 * j + n) % 6) * 512
                    act.activation(TR[:, j % 4, n * 510:(n + 1) * 510], PS[0:P, bank:bank + 510], ACT.Copy)\
                        .then_inc(S("rel_act"), 1)
            narrow("rel")
            root("ln4")
            for n in range((J + 3) // 4):
                act.wait_ge(S("t3"), n + 1)
                w = min(4, J - 4 * n) * P
                act.activation(nodeT[:, n * 500:n * 500 + w], PS[0:F, (n % 2) * 512:(n % 2) * 512 + w],
                               ACT.Copy).then_inc(S("t3_ev"), 1)
            for n in range((J + 2) // 3):
                act.wait_ge(S("nn_mm"), n + 1)
                w = min(3, J - 3 * n)
                bank = 1024 + (n % 2) * 512
                ins = act.activation(TP[:, 3 * n:3 * n + w, :],
                                     PS[0:P, bank:bank + w * (PW + F)].rearrange("p (j c) -> p j c", j=w), ACT.Copy)
                ins.then_inc(S("nn_ev"), 1)
            act.wait_ge(S("nn_ev"), (J + 2) // 3)
            act.activation(tmp2[:, :, :], TP[:, :, PW:PW + F], ACT.Copy).then_inc(S("nn_rows"), 1)
            narrow("nn")

        @block.tensor
        def _(pe):
            pe.wait_ge(S("cst"), 1)
            pe.wait_ge(S("id"), 2)
            pe.wait_ge(S("l_w"), 16 * 11)
            pe.wait_ge(S("bnd"), 1)
            pe.matmul(PS[0:P, 0:P], ones[0:1, 0:P], small[0:1, 400:400 + P], start=True, stop=True).then_inc(S("bnd_b"), 1)
            pe.wait_ge(S("wa2"), 1)
            pe.matmul(PS[0:F, 512:515], small[0:F, 0:F], small[0:F, 16:19], start=True, stop=True)
            pe.matmul(PS[0:P, 1024:1024 + F], carryT[0:F, 0:P], small[0:F, 0:F], start=True, stop=True).then_inc(S("gate_v"), 1)
            pe.wait_ge(S("wa3"), 1)
            pe.matmul(PS[0:P, 1536:1536 + F], carryT[0:F, 0:P], small[0:F, 0:F], start=True, stop=True).then_inc(S("gate_v"), 1)
            pe.transpose(PS[0:NB, 2048:2048 + R], small[0:R, 32:32 + NB], ident[0:R, 0:R]).then_inc(S("wct"), 1)
            pe.wait_ge(S("wct_c"), 1)
            pe.matmul(PS[0:R, 2560:2560 + F * F], small[0:NB, 480:480 + R], small[0:NB, 64:64 + F * F],
                      start=True, stop=True).then_inc(S("wrel_p"), 1)
            pe.wait_ge(S("diag"), 1)
            pe.matmul(PS[:, 3072:3072 + P], ones[0:P, :], diag[:, :], start=True, stop=True).then_inc(S("run_p"), 1)
            pe.wait_ge(S("setup"), 1)

            def carries(L, slot):
                w = WIDTH[L]
                pe.wait_ge(S("n_run"), upto(L, "run", NBL))
                tail = SR[:, slot * BL * w:(slot + 1) * BL * w].rearrange("p (t f) -> p t f", f=w)[:, BL - 1, :]
                pe.transpose(PS[0:w, 3072:3072 + P], tail, ident[0:P, 0:P]).then_inc(S("n_tt"), 1)
                pe.wait_ge(S("n_cs"), upto(L, "cs", 1))
                pe.transpose(PS[0:P, 3584:3584 + w], carryT[0:w, 0:P], ident[0:w, 0:w]).then_inc(S("n_cb"), 1)

            def node_transposes(sem, ready):
                pe.wait_ge(S(ready), 1)
                for n in range((J + 3) // 4):
                    if n >= 2:
                        pe.wait_ge(S(sem + "_ev"), n - 1)
                    for j in range(4 * n, min(4 * n + 4, J)):
                        ins = pe.transpose(PS[0:F, (n % 2) * 512 + (j % 4) * P:(n % 2) * 512 + (j % 4 + 1) * P],
                                           h[:, j, :], ident[0:P, 0:P])
                    ins.then_inc(S(sem), 1)

            def split_tr(b, s, k, first):
                pe.wait_ge(S("split"), b + 1)
                for g in range(5):
                    i = 5 * s + g
                    if not first or i >= 2:
                        pe.wait_ge(S("x6_ev"), 5 * b + g - 1)
                    bank = PS[0:KX, (i % 2) * 1024:(i % 2) * 1024 + B1 * 64].bitcast(bf16)\
                        .rearrange("p (t c) -> p t c", t=B1)
                    for t in range(B1):
                        ins = pe.transpose(bank[:, t, 0:P], X6[:, g * B1 + t, 0:KX], identb[0:P, 0:P])
                    ins.then_inc(S("x6_tr"), 1)

            blocks(split_tr, HALF, pe.Fori)
            pe.wait_ge(S("x6_ev"), 5 * NBL)
            carries("conv1", 0)
            node_transposes("t1", "agg1")
            for n in range((J + 3) // 4):
                pe.wait_ge(S("t1_ev"), n + 1)
                if n >= 2:
                    pe.wait_ge(S("hid_ev"), n - 1)
                w = min(4, J - 4 * n) * P
                pe.matmul(PS[0:2 * F, 1024 + (n % 2) * 512:1024 + (n % 2) * 512 + w], w1[:, :],
                          nodeT[:, n * 500:n * 500 + w], start=True, stop=True).then_inc(S("hid"), 1)
            pe.wait_ge(S("hid_ev"), (J + 3) // 4)
            for j in range(J):
                at = 2048 + (j // 32) * 512 + (j % 32) * F
                ins = pe.matmul(PS[0:P, at:at + F], HT32[:, j * P:(j + 1) * P], w2[:, :], start=True, stop=True)
            ins.then_inc(S("conv2_in"), 1)
            carries("conv2", 0)
            pe.wait_ge(S("l_w6"), 16 * 9)

            def soft(b, s, k, first):
                pe.wait_ge(S(f"soft_x{s}"), 16 * (k + 1))
                for g, n in enumerate((4, 4, 2)):
                    bank = ((g + s) % 2) * 4
                    if not first or 3 * s + g >= 2:
                        pe.wait_ge(S("soft_prod"), 3 * b + g - 1)
                    for t in range(n):
                        c = 4 * g + t
                        ins = pe.matmul(PS[0:P, (bank + t) * 512:(bank + t + 1) * 512], XT[:, s, c * P:(c + 1) * P],
                                        W6[:, :], start=True, stop=True)
                    ins.then_inc(S("soft_mm"), 1)

            blocks(soft, HALF1, pe.Fori)
            pe.wait_ge(S("soft_done"), NB1)
            for a in range(6):
                ins = pe.transpose(PS[:, (a // 4) * 512 + (a % 4) * 128:(a // 4) * 512 + (a % 4) * 128 + P],
                                   XS[:, 0, B1 - 1, a * 128:(a + 1) * 128], ident[0:P, 0:P])
            ins.then_inc(S("ct"), 1)
            pe.wait_ge(S("cc"), 1)
            for a in range(6):
                ins = pe.transpose(PS[0:P, 1024 + a * 128:1024 + (a + 1) * 128], YT[:, a, 0:P], ident[:, :])
            ins.then_inc(S("cbk"), 1)
            node_transposes("t2", "h_rel")
            pe.wait_ge(S("l_wk"), 16)
            pe.wait_ge(S("wk_gate"), 1)
            pe.wait_ge(S("t2_ev"), (J + 3) // 4)
            for j in range(J):
                for n in range(3):
                    i = 3 * j + n
                    if j >= 2 and n < 2:
                        pe.wait_ge(S("rel_act"), 2 * (j - 2) + n + 1)
                    if j >= 2 and n == 2:
                        pe.wait_ge(S("rel_evd"), j - 1)
                    bank = 1024 + (i % 6) * 512
                    pe.matmul(PS[0:P, bank:bank + 510], nodeT[:, j * P:(j + 1) * P], wk[:, n * 510:(n + 1) * 510],
                              start=True, stop=True).then_inc(S("rel_mm"), 1)
            pe.wait_ge(S("rel_act"), 2 * J)
            pe.wait_ge(S("rel_evd"), J)
            carries("rel", 0)
            node_transposes("t3", "h_nn")
            pe.wait_ge(S("l_w3"), 16 * 10)
            pe.wait_ge(S("t3_ev"), (J + 3) // 4)
            for n in range((J + 2) // 3):
                if n >= 2:
                    pe.wait_ge(S("nn_ev"), n - 1)
                for j in range(3 * n, min(3 * n + 3, J)):
                    at = 1024 + (n % 2) * 512 + (j % 3) * (PW + F)
                    ins = pe.matmul(PS[0:P, at:at + PW + F], nodeT[:, j * P:(j + 1) * P], wk[:, 0:PW + F],
                                    start=True, stop=True)
                ins.then_inc(S("nn_mm"), 1)
            carries("nn", 0)

        @block.vector
        def _(dve):
            v = nc.vector
            count = [0]

            def link(ins):
                count[0] += 1
                ins.then_inc(S("dve"), 1)
                dve.wait_ge(S("dve"), count[0])

            def bc(ap, n):
                return ap.unsqueeze(2).broadcast_to([ap.shape[0], ap.shape[1], n])

            def mid(ap, n):
                return ap.unsqueeze(1).broadcast_to([ap.shape[0], n, ap.shape[1]])

            v.memset(nextd[:, C - 1:C], -1)
            link(v.memset(ones[:, :], 1.0))
            link(v.memset(hv[:, 3:4], float(E)))
            dve.wait_ge(S("pw"), 1)
            v.memset(small[0:P, 620:621], 0.0).then_inc(S("cst"), 1)
            dve.wait_ge(S("id"), 2)
            v.tensor_copy(identb[:, :], ident[:, :])
            dve.wait_ge(S("l_dst"), 16)
            v.tensor_copy(subi, dsti.rearrange("p (k w) -> p k w", w=SUBW)[:, :, 0]).then_inc(S("sub"), 1)
            dve.wait_ge(S("iota"), 2)
            link(v.tensor_copy(ncol[:, :], qi[:, :]))
            dve.wait_ge(S("l_nb"), 64)
            link(v.tensor_tensor(keep[:, :], dsti, prevd, ALU.is_equal))
            v.tensor_copy(KR0[:, :, 1], keep[:, :])
            v.tensor_scalar(KR0[:, :, 0], keep[:, :], 1.0, BIG, ALU.subtract, ALU.mult)
            link(v.tensor_reduce(one_run[:, :], keep[:, :], X, ALU.min))
            link(v.tensor_tensor(fend, dsti, nextd, ALU.is_equal))
            link(v.scalar_tensor_tensor(iend, fend, FAR, dsti, ALU.mult, ALU.add))
            dve.wait_ge(S("l_st"), 32)
            link(v.scalar_tensor_tensor(irel, srci, float(R), typi, ALU.mult, ALU.add))
            v.memset(small[0:P, 621:622], 0.0).then_inc(S("krs"), 1)
            dve.wait_ge(S("l_bnd"), 16)
            v.tensor_copy(small[0:1, 400:400 + P], small[0:1, 400:400 + P].bitcast(i32)).then_inc(S("bnd"), 1)
            dve.wait_ge(S("bnd_b"), 1)
            w3 = wide.rearrange("p (j q) -> p j q", j=J)
            link(v.tensor_tensor(w3, mid(PS[0:P, 0:P], J), bc(ncol[:, :], P), ALU.is_lt))
            link(v.tensor_reduce(qf[:, :], w3, X, ALU.add))
            link(v.tensor_scalar(qf[:, :], qf[:, :], 1.0, 0.0, ALU.subtract, ALU.max))
            v.tensor_copy(qi[:, :], qf[:, :]).then_inc(S("q1"), 1)
            dve.wait_ge(S("g_sub"), 16 * J)
            g2v = g2.rearrange("p (j q) -> p j q", j=J)
            w2v = wide[:, 0:J * SUB].rearrange("p (j q) -> p j q", j=J)
            link(v.tensor_tensor(w2v, g2v, bc(ncol[:, :], SUB), ALU.is_lt))
            link(v.tensor_reduce(rp[:, :], w2v, X, ALU.add))
            link(v.tensor_scalar(rp[:, :], rp[:, :], 1.0, 0.0, ALU.subtract, ALU.max))
            link(v.scalar_tensor_tensor(qf[:, :], qf[:, :], float(SUB), rp[:, :], ALU.mult, ALU.add))
            v.tensor_copy(si[:, :], qf[:, :]).then_inc(S("q2"), 1)
            dve.wait_ge(S("g_row"), 16 * J)
            g3v = g3.rearrange("p (j q) -> p j q", j=J)
            w4v = wide[:, 0:J * SUBW].rearrange("p (j q) -> p j q", j=J)
            link(v.tensor_tensor(w4v, g3v, bc(ncol[:, :], SUBW), ALU.is_lt))
            link(v.tensor_reduce(st1[:, :], w4v, X, ALU.add))
            v.scalar_tensor_tensor(rp[:, :], qf[:, :], float(SUBW), st1[:, :], ALU.mult, ALU.add).then_inc(S("rp"), 1)
            dve.wait_ge(S("l_rpn"), 16)
            link(v.tensor_scalar(st2[:, :], rpn[:, :], 1.0, 0.0, ALU.subtract, ALU.max))
            v.tensor_copy(endpos[:, :], st2[:, :]).then_inc(S("endpos"), 1)
            dve.wait_ge(S("rp"), 1)
            link(v.tensor_tensor(qf[:, :], rpn[:, :], rp[:, :], ALU.subtract))
            link(v.tensor_scalar(has[:, :], qf[:, :], 0.5, None, ALU.is_gt))
            v.tensor_scalar(st1[:, :], qf[:, :], 1.0, None, ALU.add).then_inc(S("deg_var"), 1)
            dve.wait_ge(S("deg_std"), 1)
            link(v.reciprocal(dinv[:, :], st2[:, :]))

            dve.wait_ge(S("g_head"), 16)
            link(v.tensor_copy(hv[:, 0:1], head_pos[:, :]))
            link(v.tensor_copy(hv[:, 1:2], small[0:P, 600:601].bitcast(i32)))
            link(v.tensor_tensor(hv[:, 1:2], hv[:, 0:1], hv[:, 1:2], ALU.is_lt))
            link(v.tensor_tensor(hv[:, 1:2], hv[:, 1:2], keep[:, 0:1], ALU.mult))
            link(v.tensor_scalar(hv[:, 1:2], hv[:, 1:2], 1.0, -FAR, ALU.subtract, ALU.mult))
            link(v.tensor_tensor(head_row[:, :], hv[:, 1:2], hv[:, 0:1], ALU.add))
            link(v.tensor_tensor(head_node[:, :], hv[:, 1:2], dsti[:, 0:1], ALU.add))

            dve.wait_ge(S("l_w"), 16 * 11)
            v.tensor_copy(carryT[0:F, 0:P], small[0:F, 17:18].broadcast_to([F, P])).then_inc(S("wa2"), 1)
            dve.wait_ge(S("gate_v"), 1)
            gv = small[0:P, 900:900 + F]
            link(v.tensor_copy(gv, PS[0:P, 1024:1024 + F]))
            link(v.tensor_copy(wk[:, :].rearrange("i (r c) -> i r c", c=TW)[:, :, F],
                               PS[0:F, 512:513].broadcast_to([F, R])))
            v.tensor_copy(carryT[0:F, 0:P], small[0:F, 18:19].broadcast_to([F, P])).then_inc(S("wa3"), 1)
            dve.wait_ge(S("gate_v"), 2)
            link(v.tensor_copy(gdst[:, :], PS[0:P, 1536:1536 + F]))
            dve.wait_ge(S("wct"), 1)
            v.tensor_copy(small[0:NB, 480:480 + R], PS[0:NB, 2048:2048 + R]).then_inc(S("wct_c"), 1)
            dve.wait_ge(S("wrel_p"), 1)
            v.tensor_copy(small[0:R, 640:640 + F * F], PS[0:R, 2560:2560 + F * F]).then_inc(S("wrel"), 1)
            v.tensor_scalar(diag[:, :], ident[0:P, 0:P], one_run[:, 0:1], None, ALU.mult).then_inc(S("diag"), 1)
            dve.wait_ge(S("run_p"), 1)
            link(v.tensor_copy(runT[:, :], PS[:, 3072:3072 + P]))
            link(v.tensor_scalar(resT[:, :], runT[:, :], 1.0, BIG, ALU.subtract, ALU.mult))
            v.memset(small[0:P, 622:623], 0.0).then_inc(S("setup"), 1)

            def norm(name, done):
                link(v.tensor_reduce(qf[:, :], x[:, :, :], X, ALU.add))
                link(v.tensor_scalar(qf[:, :], qf[:, :], 1.0 / F, None, ALU.mult))
                link(v.tensor_tensor(h[:, :, :], x[:, :, :], bc(qf[:, :], F), ALU.subtract))
                link(v.tensor_tensor(tmp[:, :, :], h[:, :, :], h[:, :, :], ALU.mult))
                link(v.tensor_reduce(st1[:, :], tmp[:, :, :], X, ALU.add))
                v.tensor_scalar(st1[:, :], st1[:, :], 1.0 / F, EPS, ALU.mult, ALU.add).then_inc(S(f"{name}_var"), 1)
                dve.wait_ge(S(f"{name}_var"), 1)
                dve.wait_ge(S(f"{name}_std"), 1)
                link(v.reciprocal(st2[:, :], st2[:, :]))
                link(v.tensor_tensor(h[:, :, :], h[:, :, :], bc(st2[:, :], F), ALU.mult))
                ins = v.tensor_scalar(h[:, :, :], h[:, :, :], 0.0, None, ALU.max)
                if done:
                    ins.then_inc(S(done), 1)
                    dve.wait_ge(S(done), 1)
                else:
                    link(ins)

            def narrow(L):
                W, w = GROW[L], WIDTH[L]
                g = G[:, 0:2 * BL * W].rearrange("p (s t c) -> p s t c", s=2, t=BL)
                r = SR[:, 0:2 * BL * w].rearrange("p (s t c) -> p s t c", s=2, t=BL)
                m = V[:, 0:BL * F].rearrange("p (t c) -> p t c", t=BL)
                sc = V[:, BL * F:BL * F + BL]
                own = S(f"{L}_dve")

                def step(b, s, k, first):
                    dve.wait_ge(S(f"n_g{s}"), upto(L, f"g{s}", 16 * BL * (k + 1)))
                    if not first or b > 0:
                        dve.wait_ge(S("n_run"), upto(L, "run", b))
                    if not first:
                        dve.wait_ge(S(f"n_r{s}"), upto(L, f"r{s}", 16 * k))
                    if L == "rel":
                        v.tensor_tensor(sc, g[:, s, :, F], gate_e[:, bass.ds(b * BL, BL)], ALU.add).then_inc(own, 1)
                        dve.wait_ge(own, 2 * b + 1)
                        v.tensor_tensor(m, g[:, s, :, 0:F], bc(sc, F), ALU.mult).then_inc(own, 1)
                        dve.wait_ge(own, 2 * b + 2)
                    if L == "nn":
                        tm = TM.rearrange("p (t c k) -> p t c k", t=BL, k=D8)
                        dve.wait_ge(S(f"ea8_{s}"), 16 * (k + 1))
                        e8 = EA[:, s * BL * D8:(s + 1) * BL * D8].rearrange("p (t k) -> p t k", k=D8)
                        v.tensor_tensor(tm, g[:, s, :, 0:F * D8].rearrange("p t (c k) -> p t c k", k=D8),
                                        e8.unsqueeze(2).broadcast_to([P, BL, F, D8]), ALU.mult).then_inc(own, 1)
                        dve.wait_ge(own, 3 * b + 1)
                        v.tensor_reduce(m, tm, X, ALU.add).then_inc(own, 1)
                        dve.wait_ge(own, 3 * b + 2)
                        v.tensor_tensor(m, m, g[:, s, :, F * D8:PW], ALU.add).then_inc(own, 1)
                        dve.wait_ge(own, 3 * b + 3)
                    kb = keep[:, bass.ds(b * BL, BL)]
                    for f in range(w):
                        if L == "rel":
                            data = m[:, :, f] if f < F else g[:, s, :, f - F]
                        else:
                            data = m[:, :, f] if L == "nn" else g[:, s, :, f]
                        zero_start = first and s == 0
                        ins = v.tensor_tensor_scan(r[:, s, :, f], kb, data,
                                                   0.0 if zero_start else r[:, 1 - s, BL - 1:BL, f], ALU.mult, ALU.add)
                    ins.then_inc(S("n_run"), 1)
                    dve.wait_ge(S("n_run"), upto(L, "run", b + 1))
                    v.memset(small[0:1, 624:625], 0.0).then_inc(S("n_used"), 1)
                    if L == "conv1":
                        dve.wait_ge(S(f"ea16_{s}"), 16 * (k + 1))
                        if not first or b > 0:
                            dve.wait_ge(S("x6_tr"), 5 * b)
                        a = EA[:, s * BL * F:(s + 1) * BL * F].rearrange("p (t f) -> p t f", f=F)
                        n = [0]

                        def own_link(i):
                            n[0] += 1
                            i.then_inc(own, 1)
                            dve.wait_ge(own, 9 * b + n[0])

                        own_link(v.tensor_copy(X6[:, :, 0:F], a))
                        v.tensor_copy(X6[:, :, F:3 * F].rearrange("p t (a f) -> p t a f", a=2),
                                      X6[:, :, 0:F].unsqueeze(2).broadcast_to([P, BL, 2, F]))
                        own_link(v.tensor_tensor(r1, a, X6[:, :, 0:F], ALU.subtract))
                        own_link(v.tensor_copy(X6[:, :, 3 * F:4 * F], r1))
                        own_link(v.tensor_copy(X6[:, :, 4 * F:5 * F], X6[:, :, 3 * F:4 * F]))
                        own_link(v.tensor_tensor(r2, r1, X6[:, :, 3 * F:4 * F], ALU.subtract))
                        own_link(v.tensor_copy(X6[:, :, 5 * F:6 * F], r2))
                        own_link(v.memset(X6[:, :, 6 * F:6 * F + 4], 1.0))
                        own_link(v.tensor_tensor(r1, a, mid(gv, BL), ALU.mult))
                        own_link(v.tensor_reduce(gate_e[:, bass.ds(b * BL, BL)], r1, X, ALU.add))
                        v.memset(small[0:1, 626:627], 0.0).then_inc(S("split"), 1)
                        dve.wait_ge(S("split"), b + 1)

                blocks(step, HALF, dve.Fori)
                link(v.memset(carryT[:, 0:1], 0.0))
                dve.wait_ge(S("n_tt"), upto(L, "tt", 1))
                link(v.tensor_copy(small[0:w, 920:920 + P], PS[0:w, 3072:3072 + P]))
                link(v.tensor_tensor_scan(carryT[0:w, 1:P + 1], runT[0:w, :], small[0:w, 920:920 + P], 0.0,
                                          ALU.mult, ALU.add))
                v.memset(small[0:1, 627:628], 0.0).then_inc(S("n_cs"), 1)
                dve.wait_ge(S("n_cb"), upto(L, "cb", 1))
                dve.wait_ge(S("n_hg"), upto(L, "hg", 16))
                v.tensor_tensor(headb[:, 0:w], headb[:, 0:w], PS[0:P, 3584:3584 + w], ALU.add).then_inc(S("n_merged"), 1)
                dve.wait_ge(S("n_ns"), upto(L, "ns", 16 * J))
                ns = NS[:, 0:J * w].rearrange("p (j c) -> p j c", j=J)
                link(v.tensor_tensor(ns, ns, bc(has[:, :], w), ALU.mult))
                return ns

            dve.wait_ge(S("l_x"), 16)
            norm("ln1", None)
            v.tensor_tensor(h[:, :, :], h[:, :, :], bc(dinv[:, :], F), ALU.mult).then_inc(S("h_conv1"), 1)
            dve.wait_ge(S("h_conv1"), 1)
            dve.wait_ge(S("d_idx"), 48)
            dve.wait_ge(S("d_zero"), 160)
            ns = narrow("conv1")
            link(v.tensor_tensor(h[:, :, :], ns, h[:, :, :], ALU.add))
            v.tensor_tensor(h[:, :, :], h[:, :, :], bc(dinv[:, :], F), ALU.mult).then_inc(S("agg1"), 1)
            dve.wait_ge(S("conv2_in"), 1)
            for a, b in ((0, 32), (32, J)):
                ins = v.tensor_tensor(h[:, a:b, :], PS[0:P, 2048 + a * F:2048 + b * F].rearrange("p (j f) -> p j f", f=F),
                                      bc(dinv[:, a:b], F), ALU.mult)
            ins.then_inc(S("h_conv2"), 1)
            dve.wait_ge(S("h_conv2"), 1)
            ns = narrow("conv2")
            link(v.tensor_tensor(h[:, :, :], ns, h[:, :, :], ALU.add))
            link(v.tensor_tensor(h[:, :, :], h[:, :, :], bc(dinv[:, :], F), ALU.mult))
            link(v.tensor_tensor(h[:, :, :], h[:, :, :], mid(bias[:, 0, :], J), ALU.add))
            link(v.tensor_tensor(x[:, :, :], x[:, :, :], h[:, :, :], ALU.add))
            norm("ln2", "h_soft")

            v.memset(small[0:1, 628:629], 0.0).then_inc(S("conv2_nodes"), 1)
            dve.wait_ge(S("l_w1"), 64)
            for n in range(3):
                link(v.tensor_copy(W1B[:, n, :], W1F))
                if n < 2:
                    link(v.tensor_tensor(W1F, W1F, W1B[:, n, :], ALU.subtract))
                v.memset(small[0:1, 629 + n:630 + n], 0.0).then_inc(S("w1_parts"), 1)
            link(v.memset(XS[:, 1, B1 - 1, 0:CH], -BIG))
            link(v.memset(XS[:, 1, B1 - 1, CH:ROW], 0.0))

            LINKS = 3 + B1 + (B1 - 1) + 3 + 1 + 1 + 1 + B1
            own = S("soft_dve")

            def soft(b, s, k, first):
                n = [0]

                def lk(ins):
                    n[0] += 1
                    ins.then_inc(own, 1)
                    dve.wait_ge(own, b * LINKS + n[0])

                def grid(ap):
                    return ap.rearrange("p (i o) -> p i o", i=F)

                q = 1 - s
                dve.wait_ge(S(f"soft_g{s}"), 16 * B1 * (k + 1))
                dve.wait_ge(S(f"soft_k{s}"), 16 * (k + 1))
                for g, m in enumerate((4, 4, 2)):
                    bank = ((g + s) % 2) * 2048
                    dve.wait_ge(S("soft_mm"), 3 * b + g + 1)
                    v.tensor_tensor(EE[:, 4 * g:4 * g + m].rearrange("p t i c -> p (t i) c"),
                                    PS[0:P, bank:bank + m * 512].rearrange("p (a c) -> p a c", c=2 * F),
                                    bc(GH[:, s, 4 * g:4 * g + m, :].rearrange("p t i -> p (t i)"), 2 * F),
                                    ALU.mult).then_inc(S("soft_prod"), 1)
                    dve.wait_ge(S("soft_prod"), 3 * b + g + 1)
                lk(v.memset(small[0:1, 632:633], 0.0))
                lk(v.memset(small[0:1, 633:634], 0.0))
                v.memset(small[0:1, 634:635], 0.0).then_inc(S("soft_used"), 1)
                dve.wait_ge(S("soft_used"), b + 1)
                if not first:
                    dve.wait_ge(S(f"soft_s{s}"), 16 * B1 * k)
                for t in range(B1):
                    prev = XS[:, s, t - 1, 0:CH] if t else XS[:, q, B1 - 1, 0:CH]
                    lk(v.scalar_tensor_tensor(grid(XS[:, s, t, 0:CH]), grid(prev), KR[:, s, t, 0:1], EE[:, t, :, 0:F],
                                              ALU.add, ALU.max))
                for t in range(B1 - 2, -1, -1):
                    lk(v.scalar_tensor_tensor(XS[:, s, t, 0:CH], XS[:, s, t + 1, 0:CH], KR[:, s, t + 1, 0:1],
                                              XS[:, s, t, 0:CH], ALU.add, ALU.max))
                for part in range(2):
                    a = 5 * part
                    v.tensor_tensor(XS[:, s, a:a + 5, CH:2 * CH].rearrange("p t (i o) -> p t i o", i=F),
                                    EE[:, a:a + 5, :, 0:F], XS[:, s, a:a + 5, 0:CH].rearrange("p t (i o) -> p t i o", i=F),
                                    ALU.subtract).then_inc(S("soft_d"), 1)
                    if part == 0:
                        lk(v.scalar_tensor_tensor(DC, XS[:, q, B1 - 1, 0:CH], KR[:, s, 0, 0:1], XS[:, s, 0, 0:CH],
                                                  ALU.add, ALU.subtract))
                for part in range(2):
                    a = 5 * part
                    dve.wait_ge(S("soft_exp"), 3 * b + part + 1)
                    lk(v.tensor_tensor(XS[:, s, a:a + 5, 2 * CH:ROW].rearrange("p t (i o) -> p t i o", i=F),
                                       XS[:, s, a:a + 5, CH:2 * CH].rearrange("p t (i o) -> p t i o", i=F),
                                       EE[:, a:a + 5, :, F:2 * F], ALU.mult))
                dve.wait_ge(S("soft_exp"), 3 * b + 3)
                lk(v.tensor_tensor(SC, XS[:, q, B1 - 1, CH:ROW].rearrange("p (a c) -> p a c", a=2), mid(DC, 2), ALU.mult))
                for t in range(B1):
                    to = XS[:, s, t, CH:ROW]
                    if t == 0:
                        lk(v.tensor_tensor(to, to, SC.rearrange("p a c -> p (a c)"), ALU.add))
                    else:
                        lk(v.scalar_tensor_tensor(to, XS[:, s, t - 1, CH:ROW], KR[:, s, t, 1:2], to, ALU.mult, ALU.add))
                while n[0] < LINKS:
                    lk(v.memset(small[0:1, 635:636], 0.0))
                assert n[0] == LINKS
                v.memset(small[0:1, 636:637], 0.0).then_inc(S("soft_done"), 1)

            blocks(soft, HALF1, dve.Fori)
            dve.wait_ge(S("ct"), 1)
            v.tensor_copy(CT[:, 0:4, :], PS[:, 0:512].rearrange("p (a c) -> p a c", a=4)[:, :, 0:P])
            link(v.tensor_copy(CT[:, 4:6, :], PS[:, 512:768].rearrange("p (a c) -> p a c", a=2)[:, :, 0:P]))
            v.memset(YT[:, 0:2, 0:1], -BIG)
            link(v.memset(YT[:, 2:6, 0:1], 0.0))
            for a in range(2):
                link(v.tensor_tensor_scan(YT[:, a, 1:P + 1], resT[:, :], CT[:, a, :], -BIG, ALU.add, ALU.max))
                link(v.tensor_tensor(FT[:, a, :], YT[:, a, 0:P], resT[:, :], ALU.add))
                link(v.tensor_tensor(FT[:, a, :], FT[:, a, :], YT[:, a, 1:P + 1], ALU.subtract))
                v.tensor_tensor(FT[:, 2 + a, :], CT[:, a, :], YT[:, a, 1:P + 1], ALU.subtract).then_inc(S("cd"), 1)
            dve.wait_ge(S("ce"), 1)
            for a in range(2):
                for n in (2, 4):
                    link(v.tensor_tensor(CT[:, n + a, :], CT[:, n + a, :], FT[:, 2 + a, :], ALU.mult))
                    link(v.tensor_tensor_scan(YT[:, n + a, 1:P + 1], FT[:, a, :], CT[:, n + a, :], 0.0, ALU.mult, ALU.add))
            v.memset(small[0:1, 637:638], 0.0).then_inc(S("cc"), 1)
            dve.wait_ge(S("cbk"), 1)
            link(v.tensor_copy(CB, PS[0:P, 1024:1024 + ROW]))
            dve.wait_ge(S("soft_hg"), 16)
            link(v.tensor_tensor(HM[:, 2, :], HG[:, 0:CH], CB[:, 0:CH], ALU.max))
            v.tensor_tensor(HM[:, 0, :], HG[:, 0:CH], HM[:, 2, :], ALU.subtract)
            link(v.tensor_tensor(HM[:, 1, :], CB[:, 0:CH], HM[:, 2, :], ALU.subtract))
            v.memset(small[0:1, 638:639], 0.0).then_inc(S("hd"), 1)
            dve.wait_ge(S("he"), 1)
            for part, m in ((HG, 0), (CB, 1)):
                two = part[:, CH:ROW].rearrange("p (a c) -> p a c", a=2)
                link(v.tensor_tensor(two, two, mid(HM[:, m, :], 2), ALU.mult))
            link(v.tensor_tensor(HG[:, CH:ROW], HG[:, CH:ROW], CB[:, CH:ROW], ALU.add))
            v.tensor_copy(HG[:, 0:CH], HM[:, 2, :]).then_inc(S("soft_merged"), 1)
            for n in range(J // 5):
                dve.wait_ge(S(f"soft_l{n % 2}"), 16 * (n // 2 + 1))
                rows = NODE[:, n % 2]
                link(v.tensor_scalar(rows[:, :, 0:CH], rows[:, :, CH:2 * CH], 1e-30, None, ALU.max))
                link(v.reciprocal(rows[:, :, 0:CH], rows[:, :, 0:CH]))
                link(v.tensor_tensor(rows[:, :, 0:CH], rows[:, :, 0:CH], rows[:, :, 2 * CH:ROW], ALU.mult))
                v.tensor_reduce(tmp[:, 5 * n:5 * n + 5, :], rows[:, :, 0:CH].rearrange("p j (i o) -> p j o i", i=F),
                                X, ALU.add).then_inc(S("soft_n"), 1)
                dve.wait_ge(S("soft_n"), n + 1)
            link(v.tensor_tensor(x[:, :, :], x[:, :, :], tmp[:, :, :], ALU.add))
            norm("ln3", "h_rel")

            v.memset(small[0:1, 639:640], 0.0).then_inc(S("wk_gate"), 1)
            link(v.tensor_tensor(tmp[:, :, :], h[:, :, :], mid(gdst[:, :], J), ALU.mult))
            link(v.tensor_reduce(qf[:, :], tmp[:, :, :], X, ALU.add))
            for j in range(J):
                dve.wait_ge(S("rel_mm"), 3 * j + 3)
                if j >= 4:
                    dve.wait_ge(S(f"rel_t{j % 4}"), 16 * (j // 4))
                bank = 1024 + ((3 * j + 2) % 6) * 512
                v.tensor_copy(TR[:, j % 4, 1020:1530], PS[0:P, bank:bank + 510]).then_inc(S("rel_evd"), 1)
            for s in range(4):
                dve.wait_ge(S(f"rel_t{s}"), 16 * ((J - s + 3) // 4))
            ns = narrow("rel")
            link(v.tensor_tensor(tmp[:, :, :], ns[:, :, F:2 * F], bc(qf[:, :], F), ALU.mult))
            link(v.tensor_tensor(tmp[:, :, :], tmp[:, :, :], ns[:, :, 0:F], ALU.add))
            v.tensor_tensor(x[:, :, :], x[:, :, :], tmp[:, :, :], ALU.add).then_inc(S("rel_nodes"), 1)
            dve.wait_ge(S("rel_nodes"), 1)
            norm("ln4", "h_nn")

            dve.wait_ge(S("nn_rows"), 1)
            link(v.tensor_tensor(x[:, :, :], x[:, :, :], tmp2[:, :, :], ALU.add))
            link(v.tensor_tensor(x[:, :, :], x[:, :, :], mid(bias[:, 1, :], J), ALU.add))
            dve.wait_ge(S("tab_nn"), 16)
            ns = narrow("nn")
            v.tensor_tensor(x[:, :, :], x[:, :, :], ns, ALU.add).then_inc(S("x_out"), 1)


_OUTS = [((N, F), 'float32')]


def kernel(**inputs):
    import numpy as _np
    import concourse.bacc as _bacc
    from concourse import mybir as _mybir
    from concourse.bass_utils import run_bass_kernel_spmd as _run

    nc = _bacc.Bacc("TRN2", target_bir_lowering=False, num_devices=1)
    arrays, args = {}, {}
    for name in sorted(inputs):
        a = _np.ascontiguousarray(inputs[name])
        arrays[f"in_{name}"] = a
        args[name] = nc.dram_tensor(f"in_{name}", a.shape, _mybir.dt.from_np(a.dtype), kind="ExternalInput").ap()
    out = nc.dram_tensor("out_0", _OUTS[0][0], _mybir.dt.float32, kind="ExternalOutput").ap()
    graph_layers(nc, args, out)
    r = _run(nc, [arrays], core_ids=[0])
    return r.results[0]["out_0"]
```

```python
import concourse.bass as bass
from concourse import mybir
from contextlib import ExitStack

N, E, F = 6250, 206250, 16
P = 125
C = E // P
J = N // P
R = 90
NB = 30
D8 = 8
BL = 50
NBL = C // BL
HALF = (NBL - 1) // 2
B1 = 10
NB1 = C // B1
THIRD = NB1 // 3
GROUPS = (3, 3, 3, 1)
SUB = 33
SUBW = C // SUB
MAXES = 2 * B1 - 1
CH = F * F
ROW = 3 * CH
AR = 41600
KX = 6 * F + 3
TW = F + 1
PW = F * D8 + F
BIG = 1e38
FAR = 1.0e6
EPS = 1e-5
NARROW = ("conv1", "conv2", "rel", "nn")
WIDTH = {"conv1": F, "conv2": F, "rel": 2 * F, "nn": F}
GROW = {"conv1": F, "conv2": F, "rel": TW, "nn": PW}


def graph_layers(nc, A, out):
    f32, i32, bf16 = mybir.dt.float32, mybir.dt.int32, mybir.dt.bfloat16
    ALU, ACT, AX = mybir.AluOpType, mybir.ActivationFunctionType, mybir.AxisListType
    X = AX.X

    ctx = ExitStack()
    with ctx:
        def sb(name, shape, dt=f32):
            return ctx.enter_context(nc.sbuf_tensor(name, shape, dt))

        def dram(name, shape, dt=f32):
            return nc.dram_tensor(name, shape, dt).ap()

        sems = {}

        def S(name):
            if name not in sems:
                sems[name] = ctx.enter_context(nc.semaphore(name))
            return sems[name]

        total = {"i0": 16 * (HALF + 1), "i1": 16 * HALF, "g0": 16 * BL * (HALF + 1), "g1": 16 * BL * HALF,
                 "r0": 16 * (HALF + 1), "r1": 16 * HALF, "run": NBL, "hg": 16, "hs": 16,
                 "ns": 16 * J, "merged": 1, "tt": 1, "cs": 1, "cb": 1}

        def upto(L, key, value):
            return value + NARROW.index(L) * total[key]

        x = sb("x", [P, J, F])
        h = sb("h", [P, J, F])
        tmp = sb("tmp", [P, J, F])
        tmp2 = sb("tmp2", [P, J, F])
        st1 = sb("st1", [P, J])
        st2 = sb("st2", [P, J])
        keep = sb("keep", [P, C])
        gate_e = sb("gate_e", [P, C])
        dinv = sb("dinv", [P, J])
        has = sb("has", [P, J])
        ncol = sb("ncol", [P, J])
        rp = sb("rp", [P, J])
        rpn = sb("rpn", [P, J])
        qf = sb("qf", [P, J])
        endpos = sb("endpos", [P, J], i32)
        qi = sb("qi", [P, J], i32)
        si = sb("si", [P, J], i32)
        first_dst = sb("first_dst", [P, 1], i32)
        head_pos = sb("head_pos", [P, 1], i32)
        head_row = sb("head_row", [P, 1], i32)
        head_node = sb("head_node", [P, 1], i32)
        hv = sb("hv", [P, 4])
        one_run = sb("one_run", [P, 1])
        ident = sb("ident", [128, 128])
        identb = sb("identb", [128, 128], bf16)
        ones = sb("ones", [128, 128])
        diag = sb("diag", [P, P])
        runT = sb("runT", [128, P])
        resT = sb("resT", [128, P])
        small = sb("small", [128, 1060])
        wk = sb("wk", [F, R * TW])
        w1 = sb("w1", [F, 2 * F])
        w2 = sb("w2", [2 * F, F])
        bias = sb("bias", [P, 3, F])
        b1c = sb("b1c", [2 * F, 1])
        gdst = sb("gdst", [P, F])
        src_slot = sb("src_slot", [P, 2, BL], i32)
        carryT = sb("carryT", [128, 128])
        headb = sb("headb", [P, 2 * F])
        poolw = sb("poolw", [1, 2])
        arena = sb("arena", [128, AR])

        def ar(a, n):
            return arena[0:P, a:a + n]

        G = ar(0, 2 * BL * PW)
        o = 2 * BL * PW
        V = ar(o, BL * 2 * F); o += BL * 2 * F
        TM = ar(o, BL * F * D8); o += BL * F * D8
        SR = ar(o, 2 * BL * 2 * F); o += 2 * BL * 2 * F
        EA = ar(o, 2 * BL * F); o += 2 * BL * F
        assert o <= AR
        X6 = ar(4 * BL * F, BL * 50).bitcast(bf16).rearrange("p (c k) -> p c k", k=100)
        r1 = ar(TM_AT := 2 * BL * PW + BL * 2 * F, BL * F).rearrange("p (c f) -> p c f", f=F)
        r2 = ar(TM_AT + BL * F, BL * F).rearrange("p (c f) -> p c f", f=F)
        X6T = arena[0:KX, 6000:6000 + 2 * B1 * P // 2].bitcast(bf16).rearrange("p (s c) -> p s c", s=2)
        o = 0
        XS = ar(o, 3 * B1 * ROW).rearrange("p (s t c) -> p s t c", s=3, t=B1); o += 3 * B1 * ROW
        GH = ar(o, 3 * B1 * F).rearrange("p (s t f) -> p s t f", s=3, t=B1); o += 3 * B1 * F
        XT = arena[0:KX, o:o + 3 * B1 * P // 2].bitcast(bf16).rearrange("p (s c) -> p s c", s=3); o += 3 * B1 * P // 2
        W6 = arena[0:KX, o:o + CH].bitcast(bf16); o += CH
        KR = ar(o, 3 * 2 * B1).rearrange("p (s t k) -> p s t k", s=3, k=2); o += 6 * B1
        END = ar(o, 3 * B1).bitcast(i32).rearrange("p (s t) -> p s t", s=3); o += 3 * B1
        SRC1 = ar(o, 3 * B1).bitcast(i32).rearrange("p (s t) -> p s t", s=3); o += 3 * B1
        neg = ar(o, P); o += P
        DC = ar(o, CH); o += CH
        SC = ar(o, 2 * CH).rearrange("p (a c) -> p a c", a=2); o += 2 * CH
        CT = arena[:, o:o + 6 * P].rearrange("p (a c) -> p a c", a=6); o += 6 * P
        YT = arena[:, o:o + 6 * 126].rearrange("p (a c) -> p a c", a=6); o += 6 * 126
        FT = arena[:, o:o + 4 * P].rearrange("p (a c) -> p a c", a=4); o += 4 * P
        CB = ar(o, ROW); o += ROW
        HG = ar(o, ROW); o += ROW
        HM = ar(o, 3 * CH).rearrange("p (a c) -> p a c", a=3); o += 3 * CH
        W1F = arena[0:F + 1, o:o + 2 * CH]; o += 2 * CH
        W1R = arena[0:F + 1, o:o + 2 * CH]; o += 2 * CH
        W1B = arena[0:F + 1, o:o + 3 * CH].bitcast(bf16).rearrange("p (a c) -> p a c", a=3); o += 3 * CH
        assert o <= AR, o
        NODE = ar(0, 2 * 5 * ROW).rearrange("p (s j c) -> p s j c", s=2, j=5)
        o = 0
        dsti = ar(o, C).bitcast(i32); o += C
        prevd = ar(o, C).bitcast(i32); o += C
        nextd = ar(o, C).bitcast(i32); o += C
        srci = ar(o, C).bitcast(i32); o += C
        typi = ar(o, C).bitcast(i32); o += C
        wide = ar(o, J * P); o += J * P
        g2 = ar(o, J * SUB).bitcast(i32); o += J * SUB
        g3 = ar(o, J * SUBW).bitcast(i32); o += J * SUBW
        KR0 = ar(o, 2 * C).rearrange("p (c k) -> p c k", k=2); o += 2 * C
        fend = ar(o, C); o += C
        iend = ar(o, C).bitcast(i32); o += C
        irel = ar(o, C).bitcast(i32); o += C
        subi = ar(o, SUB).bitcast(i32); o += SUB
        zero = ar(AR - 3840, 3840)
        o += 3840
        assert o <= AR, o
        TR = arena[0:P, 0:4 * R * TW].rearrange("p (s c) -> p s c", s=4)
        TP = arena[0:P, 0:J * (PW + F)].rearrange("p (j c) -> p j c", j=J)
        HT32 = arena[0:2 * F, 0:J * P]
        XN = ar(8000, J * 48).bitcast(bf16).rearrange("p (j k) -> p j k", k=6 * F)
        NT6 = arena[0:6 * F, 10500:10500 + J * P // 2].bitcast(bf16)
        WR6 = arena[0:6 * F, 13700:13700 + R * TW // 2].bitcast(bf16)
        WRB = arena[0:F, 14500:14500 + 3 * R * TW // 2].bitcast(bf16).rearrange("p (a c) -> p a c", a=3)
        NS = ar(20000, J * 2 * F)
        nodeT = arena[0:F, 22000:22000 + J * P]

        PS = ctx.enter_context(nc.psum_tensor("PS", [128, 4096], f32))

        d_h = dram("d_h", [N, F])
        d_sub = dram("d_sub", [P, SUB], i32)
        d_rp = dram("d_rp", [N + 1, 1])
        d_end = dram("d_end", [N, 1], i32)
        d_kr = dram("d_kr", [E, 2])
        d_iend = dram("d_iend", [E], i32)
        d_irel = dram("d_irel", [E], i32)
        d_x6 = dram("d_x6", [KX, C * P], bf16)
        d_w = dram("d_w", [F, R, F])
        d_soft = dram("d_soft", [N, ROW])
        d_rel = dram("d_rel", [N * R, TW])
        d_nn = dram("d_nn", [N, PW])
        d_run = {k: dram(f"d_run_{k}", [E, WIDTH[k]]) for k in NARROW}
        d_tab = {"conv1": d_h, "conv2": dram("d_h2", [N, F]), "rel": d_rel, "nn": d_nn}
        d_feat = dram("d_feat", [N, F])
        d_index = {"conv1": A["src"], "conv2": A["src"], "rel": d_irel, "nn": A["src"]}

        def nodes(t):
            return t.rearrange("(p j) f -> p (j f)", p=P)

        def edges(t):
            return t.rearrange("(p c) -> p c", p=P)

        def edges_w(t):
            return t.rearrange("(p c) f -> p (c f)", p=P)

        def flat(t):
            return t.rearrange("p j f -> p (j f)")

        ea16 = edges_w(A["edge_attr_16"])
        ea8 = edges_w(A["edge_attr_8"])

        def blocks(step, half, fori):
            step(0, 0, 0, True)
            step(1, 1, 0, True)
            with fori(1, half) as k:
                step(2 * k, 0, k, False)
                step(2 * k + 1, 1, k, False)
            step(2 * half, 0, half, False)

        def wide_dma(eng, to, of, sem):
            for a, b in ((0, 112), (112, P)):
                eng.dma_start(to[a:b], of[a:b]).then_inc(S(sem), 16)

        def triples(step, fori):
            for s in range(3):
                step(s, s, 0, True)
            with fori(1, THIRD) as k:
                for s in range(3):
                    step(3 * k + s, s, k, False)

        block = ctx.enter_context(nc.Block())

        @block.sync
        def _(sp):
            dst = A["dst"]
            wide_dma(sp, dsti, edges(dst), "l_dst")
            sp.wait_ge(S("cst"), 1)
            sp.dma_start(prevd[0:1, 1:C], dst[0:C - 1].rearrange("(a c) -> a c", a=1)).then_inc(S("l_nb"), 16)
            sp.dma_start(prevd[1:P, :], dst[C - 1:E - 1].rearrange("(p c) -> p c", c=C)).then_inc(S("l_nb"), 16)
            sp.dma_start(nextd[0:P - 1, :], dst[1:E - C + 1].rearrange("(p c) -> p c", c=C)).then_inc(S("l_nb"), 16)
            sp.dma_start(nextd[P - 1:P, 0:C - 1], dst[E - C + 1:E].rearrange("(a c) -> a c", a=1)).then_inc(S("l_nb"), 16)
            sp.dma_start(flat(x), nodes(A["x"])).then_inc(S("l_x"), 16)
            sp.dma_start(srci, edges(A["src"])).then_inc(S("l_st"), 16)
            sp.dma_start(typi, edges(A["edge_type_90"])).then_inc(S("l_st"), 16)
            sp.dma_start(w1[:, :], A["L0_gnn_W1"]).then_inc(S("l_w"), 16)
            sp.dma_start(w2[:, :], A["L0_gnn_W2"]).then_inc(S("l_w"), 16)
            sp.dma_start(b1c[:, :], A["L0_gnn_b1"].rearrange("(f a) -> f a", a=1)).then_inc(S("l_w"), 16)
            for n, b in enumerate(("L0_gnn_b2", "L3_gnn_root_b")):
                sp.dma_start(bias[:, n, :], A[b].partition_broadcast(P)).then_inc(S("l_w"), 16)
            sp.dma_start(small[0:F, 0:F], A["L2_gnn_Ws"]).then_inc(S("l_w"), 16)
            for n in range(3):
                sp.dma_start(small[0:F, 16 + n:17 + n],
                             A["L2_gnn_Wa"][0, n * F:(n + 1) * F].rearrange("(o a) -> o a", a=1)).then_inc(S("l_w"), 16)
            sp.dma_start(small[0:R, 32:32 + NB], A["L2_gnn_w_comp"]).then_inc(S("l_w"), 16)
            sp.dma_start(small[0:NB, 64:64 + F * F].rearrange("b (a o) -> b a o", a=F),
                         A["L2_gnn_weight"].rearrange("b i o -> (b i o)")
                         .rearrange("(a b o) -> b a o", a=F, b=NB)).then_inc(S("l_w"), 16)
            sp.wait_ge(S("sub"), 1)
            sp.dma_start(d_sub, subi).then_inc(S("d_sub"), 16)
            sp.wait_ge(S("d_sub"), 16)
            sp.dma_start(small[0:1, 400:400 + P].bitcast(i32), d_sub[:, 0:1].rearrange("p a -> a p"),
                         allow_slow_non_contiguous=True).then_inc(S("l_bnd"), 16)
            sp.wait_ge(S("zero"), 1)
            for n in range(10):
                wide_dma(sp, nodes(d_soft)[:, n * 3840:(n + 1) * 3840], zero, "d_zero")
            sp.wait_ge(S("krs"), 1)
            wide_dma(sp, edges_w(d_kr), KR0.rearrange("p c k -> p (c k)"), "d_idx")
            wide_dma(sp, edges(d_iend), iend, "d_idx")
            wide_dma(sp, edges(d_irel), irel, "d_idx")
            sp.wait_ge(S("rp"), 1)
            sp.dma_start(nodes(d_rp[0:N, :]), rp[:, :]).then_inc(S("d_rp"), 16)
            sp.dma_start(d_rp[N:N + 1, :], hv[0:1, 3:4]).then_inc(S("d_rp"), 16)
            sp.wait_ge(S("d_rp"), 32)
            sp.dma_start(rpn[:, :], nodes(d_rp[1:N + 1, :])).then_inc(S("l_rpn"), 16)
            sp.wait_ge(S("endpos"), 1)
            sp.dma_start(nodes(d_end), endpos[:, :]).then_inc(S("d_end"), 16)
            sp.wait_ge(S("h_conv1"), 1)
            sp.dma_start(nodes(d_h), flat(h)).then_inc(S("tab_conv1"), 16)
            sp.wait_ge(S("d_idx"), 96)

            def narrow(L):
                index = edges(d_index[L])

                def step(b, s, k, first):
                    if not first:
                        sp.wait_ge(S(f"n_g{s}"), upto(L, f"g{s}", 16 * BL * k))
                    sp.dma_start(src_slot[:, s, :], index[:, bass.ds(b * BL, BL)]).then_inc(S(f"n_i{s}"), 16)
                    if L == "conv1":
                        if not first:
                            sp.wait_ge(S("split"), b - 1)
                        sp.dma_start(EA[:, s * BL * F:(s + 1) * BL * F],
                                     ea16[:, bass.ds(b * (BL * F), BL * F)]).then_inc(S(f"ea16_{s}"), 16)
                    if L == "nn":
                        if not first:
                            sp.wait_ge(S("n_run"), upto(L, "run", b - 1))
                        sp.dma_start(EA[:, s * BL * D8:(s + 1) * BL * D8],
                                     ea8[:, bass.ds(b * (BL * D8), BL * D8)]).then_inc(S(f"ea8_{s}"), 16)

                blocks(step, HALF, sp.Fori)

            narrow("conv1")
            sp.wait_ge(S("h_conv2"), 1)
            sp.dma_start(nodes(d_tab["conv2"]), flat(h)).then_inc(S("tab_conv2"), 16)
            sp.wait_ge(S("n_g0"), 16 * BL * (HALF + 1))
            sp.wait_ge(S("n_g1"), 16 * BL * HALF)
            narrow("conv2")
            sp.wait_ge(S("h_soft"), 1)
            sp.wait_ge(S("d_zero"), 320)
            for n, k in enumerate(("attn", "msg")):
                w = W1F[:, n * CH:(n + 1) * CH]
                sp.dma_start(w[0:F], A[f"L1_gnn_W_{k}"]).then_inc(S("l_w1"), 16)
                sp.dma_start(w[F:F + 1], A[f"L1_gnn_b_{k}"].rearrange("(a c) -> a c", a=1)).then_inc(S("l_w1"), 16)
            sp.wait_ge(S("w1_parts"), 3)
            for n, part in enumerate((0, 1, 2, 0, 1, 0)):
                sp.dma_start(W6[n * F:(n + 1) * F, :], W1B[0:F, part, :]).then_inc(S("l_w6"), 16)
            for part in range(3):
                sp.dma_start(W6[6 * F + part:6 * F + part + 1, :], W1B[F:F + 1, part, :]).then_inc(S("l_w6"), 16)
            sp.wait_ge(S("wrel"), 1)
            sp.dma_start(d_w.rearrange("a r o -> r a o"), small[0:R, 640:896].rearrange("r (a o) -> r a o", a=F))\
                .then_inc(S("d_w"), 16)
            sp.wait_ge(S("d_w"), 16)
            sp.dma_start(wk[:, :].rearrange("i (r c) -> i r c", c=TW)[:, :, 0:F],
                         d_w.rearrange("a r o -> (a r o)").rearrange("(r i o) -> i r o", i=F, o=F)).then_inc(S("l_wk"), 16)
            sp.wait_ge(S("h_soft"), 1)
            sp.dma_start(nodes(d_feat), flat(h)).then_inc(S("tab_soft"), 16)
            sp.wait_ge(S("x6_0"), 16 * (5 * HALF + 3))
            sp.wait_ge(S("x6_1"), 16 * (5 * HALF + 2))

            def soft(b, s, k, first):
                if not first:
                    sp.wait_ge(S(f"soft_g{s}"), 16 * B1 * k)
                sp.dma_start(SRC1[:, s, :], edges(A["src"])[:, bass.ds(b * B1, B1)]).then_inc(S(f"soft_i{s}"), 16)
                if not first:
                    sp.wait_ge(S("soft_done"), b - 2)
                sp.dma_start(KR[:, s], edges_w(d_kr)[:, bass.ds(b * (2 * B1), 2 * B1)].rearrange("p (t k) -> p t k", k=2))\
                    .then_inc(S(f"soft_k{s}"), 16)
                sp.dma_start(XT[:, s, :], d_x6[:, bass.ds(b * (B1 * P), B1 * P)]).then_inc(S(f"soft_k{s}"), 16)

            triples(soft, sp.Fori)
            sp.wait_ge(S("soft_heads"), 16)
            for n in range(J // 5):
                if n >= 2:
                    sp.wait_ge(S("soft_n"), n - 1)
                wide_dma(sp, NODE[:, n % 2].rearrange("p j c -> p (j c)"),
                         nodes(d_soft)[:, n * 5 * ROW:(n + 1) * 5 * ROW], f"soft_l{n % 2}")
            sp.wait_ge(S("wk_parts"), 3)
            for n, part in enumerate((0, 1, 2, 0, 1, 0)):
                sp.dma_start(WR6[n * F:(n + 1) * F, :], WRB[:, part, :]).then_inc(S("l_w6"), 16)
            for j in range(J):
                sp.wait_ge(S("rel_act"), 2 * (j + 1))
                sp.wait_ge(S("rel_evd"), j + 1)
                wide_dma(sp, d_rel.rearrange("(p j r) c -> p j (r c)", p=P, j=J)[:, j, :], TR[:, j % 4, :],
                         f"rel_t{j % 4}")
            for s in range(4):
                sp.wait_ge(S(f"rel_t{s}"), 32 * ((J - s + 3) // 4))
            narrow("rel")
            sp.wait_ge(S("rel_nodes"), 1)
            for k in range(D8):
                sp.dma_start(wk[:, 0:F * D8].rearrange("i (o k) -> i o k", k=D8)[:, :, k:k + 1],
                             A["L3_gnn_edge_w"][k, :].rearrange("(o i) -> i o", i=F).unsqueeze(2), allow_slow_non_contiguous=True).then_inc(S("l_w3"), 16)
            sp.dma_start(wk[:, F * D8:PW].unsqueeze(2), A["L3_gnn_edge_b"].rearrange("(o i) -> i o", i=F).unsqueeze(2), allow_slow_non_contiguous=True).then_inc(S("l_w3"), 16)
            sp.dma_start(wk[:, PW:PW + F], A["L3_gnn_root_w"]).then_inc(S("l_w3"), 16)
            sp.wait_ge(S("nn_rows"), 1)
            sp.dma_start(d_nn.rearrange("(p j) c -> p j c", p=P), TP[:, :, 0:PW]).then_inc(S("tab_nn"), 16)
            sp.wait_ge(S("tab_nn"), 16)
            narrow("nn")
            sp.wait_ge(S("x_out"), 1)
            sp.dma_start(nodes(out), flat(x)).then_inc(S("out"), 16)
            sp.wait_ge(S("out"), 16)

        @block.gpsimd
        def _(gp):
            gp.memset(prevd[0:1, 0:1], -1)
            gp.memset(zero, 0.0).then_inc(S("zero"), 1)
            gp.memset(poolw[:, :], 0.0).then_inc(S("pw"), 1)
            gp.iota(qi[:, :], pattern=[[1, J]], base=0, channel_multiplier=J).then_inc(S("iota"), 1)
            gp.memset(ident[:, :], 0.0).then_inc(S("id"), 1)
            gp.wait_ge(S("id"), 1)
            gp.affine_select(out=ident[:, :], in_=ident[:, :], compare_op=ALU.not_equal, fill=1.0,
                             base=0, pattern=[[-1, 128]], channel_multiplier=1).then_inc(S("id"), 1)
            gp.iota(small[0:P, 600:601].bitcast(i32), pattern=[[1, 1]], base=C, channel_multiplier=C).then_inc(S("iota"), 1)

            def gather(dst, table, index, sem):
                gp.indirect_dma_start(out=dst, out_offset=None, in_=table,
                                      in_offset=bass.IndirectOffsetOnAxis(ap=index, axis=0)).then_inc(S(sem), 16)

            def scatter(table, index, src, sem):
                gp.indirect_dma_start(out=table, out_offset=bass.IndirectOffsetOnAxis(ap=index, axis=0), in_=src,
                                      in_offset=None, bounds_check=table.shape[0] - 1, oob_is_err=False).then_inc(S(sem), 16)

            tick = [1]

            def hold(value):
                gp.wait_ge(S("pw"), value)
                gp.tensor_tensor(poolw[:, 0:1], poolw[:, 1:2], poolw[:, 1:2], ALU.add).then_inc(S("pw"), 1)

            gp.wait_ge(S("q1"), 1)
            gp.wait_ge(S("d_sub"), 16)
            for j in range(J):
                gather(g2[:, j * SUB:(j + 1) * SUB], d_sub, qi[:, j:j + 1], "g_sub")
            gp.wait_ge(S("q2"), 1)
            rows = A["dst"].rearrange("(r w) -> r w", w=SUBW)
            for j in range(J):
                gather(g3[:, j * SUBW:(j + 1) * SUBW], rows, si[:, j:j + 1], "g_row")
            gp.wait_ge(S("d_end"), 16)
            gp.wait_ge(S("l_fd"), 16)
            gather(head_pos[:, :], d_end, first_dst[:, :], "g_head")

            def narrow(L):
                W = GROW[L]
                g = G[:, 0:2 * BL * W].rearrange("p (s t w) -> p s t w", s=2, t=BL)
                base = tick[0]

                def step(b, s, k, first):
                    gp.wait_ge(S(f"n_i{s}"), upto(L, f"i{s}", 16 * (k + 1)))
                    if not first:
                        gp.wait_ge(S("n_run"), upto(L, "run", b - 1))
                    hold(b + base)
                    for t in range(BL):
                        gather(g[:, s, t, :], d_tab[L], src_slot[:, s, t:t + 1], f"n_g{s}")

                blocks(step, HALF, gp.Fori)
                tick[0] += NBL
                w = WIDTH[L]
                gp.wait_ge(S("n_r0"), upto(L, "r0", 16 * (HALF + 1)))
                gp.wait_ge(S("n_r1"), upto(L, "r1", 16 * HALF))
                gather(headb[:, 0:w], d_run[L], head_pos[:, :], "n_hg")
                gp.wait_ge(S("n_merged"), upto(L, "merged", 1))
                scatter(d_run[L], head_row[:, :], headb[:, 0:w], "n_hs")
                gp.wait_ge(S("n_hs"), upto(L, "hs", 16))
                for j in range(J):
                    gather(NS[:, j * w:(j + 1) * w], d_run[L], endpos[:, j:j + 1], "n_ns")

            gp.wait_ge(S("tab_conv1"), 16)
            gp.wait_ge(S("d_idx"), 96)
            narrow("conv1")
            gp.wait_ge(S("tab_conv2"), 16)
            narrow("conv2")

            gp.wait_ge(S("tab_soft"), 16)
            gp.wait_ge(S("d_zero"), 320)
            base = tick[0]

            def gathers(b, s, k, held):
                gp.wait_ge(S(f"soft_i{s}"), 16 * (k + 1))
                gp.wait_ge(S("soft_prod"), 4 * (b - 2))
                hold(held)
                for t in range(B1):
                    gather(GH[:, s, t, :], d_feat, SRC1[:, s, t:t + 1], f"soft_g{s}")

            def scatters(b, s, k, held):
                gp.wait_ge(S(f"soft_e{s}"), 16 * (k + 1))
                gp.wait_ge(S("soft_done"), b + 1)
                hold(held)
                for t in range(B1):
                    scatter(d_soft, END[:, s, t:t + 1], XS[:, s, t, :], f"soft_s{s}")

            for s in range(3):
                gp.wait_ge(S(f"soft_i{s}"), 16)
                hold(base + s)
                for t in range(B1):
                    gather(GH[:, s, t, :], d_feat, SRC1[:, s, t:t + 1], f"soft_g{s}")
            with gp.Fori(0, THIRD - 1) as k:
                for s in range(3):
                    gathers(3 * k + s + 3, s, k + 1, 6 * k + (base + 3 + 2 * s))
                    scatters(3 * k + s, s, k, 6 * k + (base + 4 + 2 * s))
            for s in range(3):
                scatters(NB1 - 3 + s, s, THIRD - 1, base + 2 * NB1 - 3 + s)
            tick[0] += 2 * NB1
            for s in range(3):
                gp.wait_ge(S(f"soft_s{s}"), 16 * B1 * THIRD)
            gather(HG, d_soft, first_dst[:, :], "soft_hg")
            gp.wait_ge(S("soft_merged"), 1)
            scatter(d_soft, head_node[:, :], HG, "soft_heads")

            for s in range(4):
                gp.wait_ge(S(f"rel_t{s}"), 32 * ((J - s + 3) // 4))
            narrow("rel")
            gp.wait_ge(S("tab_nn"), 16)
            narrow("nn")

        @block.scalar
        def _(act):
            def store_runs(L):
                w = WIDTH[L]
                run = edges_w(d_run[L])
                return lambda b, s: act.dma_start(run[:, bass.ds(b * (BL * w), BL * w)],
                                                  SR[:, s * BL * w:(s + 1) * BL * w]).then_inc(S(f"n_r{s}"), 16)

            act.wait_ge(S("l_dst"), 32)
            act.dma_start(first_dst[:, :], edges(A["dst"])[:, 0:1], allow_slow_non_contiguous=True).then_inc(S("l_fd"), 16)

            def root(name):
                act.wait_ge(S(f"{name}_var"), 1)
                act.activation(st2[:, :], st1[:, :], ACT.Sqrt).then_inc(S(f"{name}_std"), 1)

            root("deg")
            root("ln1")

            def narrow(L):
                store = store_runs(L)

                def step(b, s, k, first):
                    act.wait_ge(S("n_run"), upto(L, "run", b + 1))
                    store(b, s)
                    if L == "conv1":
                        for g in range(5):
                            i = 5 * s + g
                            act.wait_ge(S("x6_tr"), 5 * b + g + 1)
                            if not first or i >= 2:
                                act.wait_ge(S(f"x6_{i % 2}"), 80 * k + 16 * (i // 2))
                            bank = PS[0:KX, (i % 2) * 1024:(i % 2) * 1024 + B1 * 64].bitcast(bf16)\
                                .rearrange("p (t c) -> p t c", t=B1)
                            act.activation(X6T[:, i % 2, :].rearrange("p (t c) -> p t c", t=B1), bank[:, :, 0:P],
                                           ACT.Copy).then_inc(S("x6_ev"), 1)
                            act.wait_ge(S("x6_ev"), 5 * b + g + 1)
                            act.dma_start(d_x6[:, bass.ds(b * (BL * P) + g * (B1 * P), B1 * P)], X6T[:, i % 2, :])\
                                .then_inc(S(f"x6_{i % 2}"), 16)

                blocks(step, HALF, act.Fori)

            narrow("conv1")
            act.wait_ge(S("x6_0"), 16 * (5 * HALF + 3))
            act.wait_ge(S("x6_1"), 16 * (5 * HALF + 2))
            for n in range((J + 3) // 4):
                act.wait_ge(S("t1"), n + 1)
                w = min(4, J - 4 * n) * P
                act.activation(nodeT[:, n * 500:n * 500 + w], PS[0:F, (n % 2) * 512:(n % 2) * 512 + w],
                               ACT.Copy).then_inc(S("t1_ev"), 1)
            act.wait_ge(S("l_w"), 16 * 10)
            for n in range((J + 3) // 4):
                act.wait_ge(S("hid"), n + 1)
                w = min(4, J - 4 * n) * P
                act.activation(HT32[:, n * 500:n * 500 + w], PS[0:2 * F, 1024 + (n % 2) * 512:1024 + (n % 2) * 512 + w],
                               ACT.Relu, bias=b1c[:, 0:1]).then_inc(S("hid_ev"), 1)
            narrow("conv2")
            root("ln2")

            def soft(b, s, k, first):
                if not first:
                    act.wait_ge(S(f"soft_s{s}"), 16 * B1 * k)
                act.dma_start(END[:, s, :], edges(d_iend)[:, bass.ds(b * B1, B1)]).then_inc(S(f"soft_e{s}"), 16)
                for n in range(6):
                    act.wait_ge(S("soft_diff"), 6 * b + n + 1)
                    bank = PS[0:P, (6 + n % 2) * 512:(7 + n % 2) * 512]
                    if n < 5:
                        t = B1 - 2 - 2 * n
                        act.activation(XS[:, s, t:t + 2, CH:2 * CH], bank.rearrange("p (t c) -> p t c", t=2), ACT.Exp)\
                           .then_inc(S("soft_exp"), 1)
                    else:
                        act.activation(DC, bank[:, 0:CH], ACT.Exp, bias=KR[:, s, 0, 0:1]).then_inc(S("soft_exp"), 1)

            act.wait_ge(S("h_soft"), 1)
            act.wait_ge(S("d_zero"), 320)
            triples(soft, act.Fori)
            act.wait_ge(S("cd"), 2)
            act.activation(FT[:, :, :], FT[:, :, :], ACT.Exp).then_inc(S("ce"), 1)
            act.wait_ge(S("hd"), 1)
            act.activation(HM[:, 0:2, :], HM[:, 0:2, :], ACT.Exp).then_inc(S("he"), 1)
            root("ln3")
            for n in range((J + 7) // 8):
                act.wait_ge(S("t2"), n + 1)
                w = min(8, J - 8 * n)
                bank = PS[0:6 * F, (n % 2) * 512:(n % 2 + 1) * 512].bitcast(bf16).rearrange("p (j c) -> p j c", j=8)
                act.activation(NT6[:, 8 * n * P:(8 * n + w) * P].rearrange("p (j c) -> p j c", c=P), bank[:, 0:w, 0:P],
                               ACT.Copy).then_inc(S("t2_ev"), 1)
            for j in range(J):
                for n in range(2):
                    act.wait_ge(S("rel_mm"), 3 * j + n + 1)
                    if j >= 4:
                        act.wait_ge(S(f"rel_t{j % 4}"), 32 * (j // 4))
                    bank = 1024 + ((3 * j + n) % 6) * 512
                    act.activation(TR[:, j % 4, n * 510:(n + 1) * 510], PS[0:P, bank:bank + 510], ACT.Copy)\
                        .then_inc(S("rel_act"), 1)
            narrow("rel")
            root("ln4")
            for n in range((J + 3) // 4):
                act.wait_ge(S("t3"), n + 1)
                w = min(4, J - 4 * n) * P
                act.activation(nodeT[:, n * 500:n * 500 + w], PS[0:F, (n % 2) * 512:(n % 2) * 512 + w],
                               ACT.Copy).then_inc(S("t3_ev"), 1)
            for n in range((J + 2) // 3):
                act.wait_ge(S("nn_mm"), n + 1)
                w = min(3, J - 3 * n)
                bank = 1024 + (n % 2) * 512
                ins = act.activation(TP[:, 3 * n:3 * n + w, :],
                                     PS[0:P, bank:bank + w * (PW + F)].rearrange("p (j c) -> p j c", j=w), ACT.Copy)
                ins.then_inc(S("nn_ev"), 1)
            act.wait_ge(S("nn_ev"), (J + 2) // 3)
            act.activation(tmp2[:, :, :], TP[:, :, PW:PW + F], ACT.Copy).then_inc(S("nn_rows"), 1)
            narrow("nn")

        @block.tensor
        def _(pe):
            pe.wait_ge(S("cst"), 1)
            pe.wait_ge(S("id"), 2)
            pe.wait_ge(S("l_w"), 16 * 11)
            pe.wait_ge(S("bnd"), 1)
            pe.matmul(PS[0:P, 0:P], ones[0:1, 0:P], small[0:1, 400:400 + P], start=True, stop=True).then_inc(S("bnd_b"), 1)
            pe.wait_ge(S("wa2"), 1)
            pe.matmul(PS[0:F, 512:515], small[0:F, 0:F], small[0:F, 16:19], start=True, stop=True)
            pe.matmul(PS[0:P, 1024:1024 + F], carryT[0:F, 0:P], small[0:F, 0:F], start=True, stop=True).then_inc(S("gate_v"), 1)
            pe.wait_ge(S("wa3"), 1)
            pe.matmul(PS[0:P, 1536:1536 + F], carryT[0:F, 0:P], small[0:F, 0:F], start=True, stop=True).then_inc(S("gate_v"), 1)
            pe.transpose(PS[0:NB, 2048:2048 + R], small[0:R, 32:32 + NB], ident[0:R, 0:R]).then_inc(S("wct"), 1)
            pe.wait_ge(S("wct_c"), 1)
            pe.matmul(PS[0:R, 2560:2560 + F * F], small[0:NB, 480:480 + R], small[0:NB, 64:64 + F * F],
                      start=True, stop=True).then_inc(S("wrel_p"), 1)
            pe.wait_ge(S("diag"), 1)
            pe.matmul(PS[:, 3072:3072 + P], ones[0:P, :], diag[:, :], start=True, stop=True).then_inc(S("run_p"), 1)
            pe.wait_ge(S("setup"), 1)

            def carries(L, slot):
                w = WIDTH[L]
                pe.wait_ge(S("n_run"), upto(L, "run", NBL))
                tail = SR[:, slot * BL * w:(slot + 1) * BL * w].rearrange("p (t f) -> p t f", f=w)[:, BL - 1, :]
                pe.transpose(PS[0:w, 3072:3072 + P], tail, ident[0:P, 0:P]).then_inc(S("n_tt"), 1)
                pe.wait_ge(S("n_cs"), upto(L, "cs", 1))
                pe.transpose(PS[0:P, 3584:3584 + w], carryT[0:w, 0:P], ident[0:w, 0:w]).then_inc(S("n_cb"), 1)

            def node_transposes(sem, ready):
                pe.wait_ge(S(ready), 1)
                for n in range((J + 3) // 4):
                    if n >= 2:
                        pe.wait_ge(S(sem + "_ev"), n - 1)
                    for j in range(4 * n, min(4 * n + 4, J)):
                        ins = pe.transpose(PS[0:F, (n % 2) * 512 + (j % 4) * P:(n % 2) * 512 + (j % 4 + 1) * P],
                                           h[:, j, :], ident[0:P, 0:P])
                    ins.then_inc(S(sem), 1)

            def split_tr(b, s, k, first):
                pe.wait_ge(S("split"), b + 1)
                for g in range(5):
                    i = 5 * s + g
                    if not first or i >= 2:
                        pe.wait_ge(S("x6_ev"), 5 * b + g - 1)
                    bank = PS[0:KX, (i % 2) * 1024:(i % 2) * 1024 + B1 * 64].bitcast(bf16)\
                        .rearrange("p (t c) -> p t c", t=B1)
                    for t in range(B1):
                        ins = pe.transpose(bank[:, t, 0:P], X6[:, g * B1 + t, 0:KX], identb[0:P, 0:P])
                    ins.then_inc(S("x6_tr"), 1)

            blocks(split_tr, HALF, pe.Fori)
            pe.wait_ge(S("x6_ev"), 5 * NBL)
            carries("conv1", 0)
            node_transposes("t1", "agg1")
            for n in range((J + 3) // 4):
                pe.wait_ge(S("t1_ev"), n + 1)
                if n >= 2:
                    pe.wait_ge(S("hid_ev"), n - 1)
                w = min(4, J - 4 * n) * P
                pe.matmul(PS[0:2 * F, 1024 + (n % 2) * 512:1024 + (n % 2) * 512 + w], w1[:, :],
                          nodeT[:, n * 500:n * 500 + w], start=True, stop=True).then_inc(S("hid"), 1)
            pe.wait_ge(S("hid_ev"), (J + 3) // 4)
            for j in range(J):
                at = 2048 + (j // 32) * 512 + (j % 32) * F
                ins = pe.matmul(PS[0:P, at:at + F], HT32[:, j * P:(j + 1) * P], w2[:, :], start=True, stop=True)
            ins.then_inc(S("conv2_in"), 1)
            carries("conv2", 0)
            pe.wait_ge(S("l_w6"), 16 * 9)

            pe.wait_ge(S("neg"), 1)

            def products(b, s, k, which):
                if 0 in which:
                    pe.wait_ge(S(f"soft_k{s}"), 32 * (k + 1))
                for g in which:
                    if not isinstance(b, int) or 4 * b + g >= 2:
                        pe.wait_ge(S("soft_prod"), 4 * b + g - 1)
                    for n in range(GROUPS[g]):
                        bank, t = 3 * (g % 2) + n, 3 * g + n
                        ins = pe.matmul(PS[0:P, bank * 512:(bank + 1) * 512], XT[:, s, t * P:(t + 1) * P],
                                        W6[:, :], start=True, stop=True)
                    ins.then_inc(S("soft_mm"), 1)

            def soft(b, s, k, first, last=False):
                if not last:
                    products(b + 1, (s + 1) % 3, k + (s == 2), (0, 1))
                for n in range(6):
                    if n == 5 and not last:
                        products(b + 1, (s + 1) % 3, k + (s == 2), (2, 3))
                    pe.wait_ge(S("soft_max"), MAXES * b + min(B1 + 1 + 2 * n, MAXES))
                    if not first or 6 * s + n >= 2:
                        pe.wait_ge(S("soft_exp"), 6 * b + n - 1)
                    bank = PS[0:P, (6 + n % 2) * 512:(7 + n % 2) * 512]
                    if n < 5:
                        t = B1 - 2 - 2 * n
                        pe.matmul(bank, ident[0:P, 0:P], XS[:, s, t:t + 2, CH:2 * CH], start=True, stop=False)
                        pe.matmul(bank, neg, XS[:, s, t:t + 2, 0:CH], start=False, stop=True).then_inc(S("soft_diff"), 1)
                    else:
                        pe.matmul(bank[:, 0:CH], ident[0:P, 0:P], XS[:, (s + 2) % 3, B1 - 1, 0:CH], start=True, stop=False)
                        pe.matmul(bank[:, 0:CH], neg, XS[:, s, 0, 0:CH], start=False, stop=True).then_inc(S("soft_diff"), 1)

            products(0, 0, 0, (0, 1, 2, 3))
            for s in range(3):
                soft(s, s, 0, True)
            with pe.Fori(1, THIRD - 1) as k:
                for s in range(3):
                    soft(3 * k + s, s, k, False)
            for s in range(3):
                soft(NB1 - 3 + s, s, THIRD - 1, False, s == 2)
            pe.wait_ge(S("soft_done"), NB1)
            for a in range(6):
                ins = pe.transpose(PS[:, (a // 4) * 512 + (a % 4) * 128:(a // 4) * 512 + (a % 4) * 128 + P],
                                   XS[:, 2, B1 - 1, a * 128:(a + 1) * 128], ident[0:P, 0:P])
            ins.then_inc(S("ct"), 1)
            pe.wait_ge(S("cc"), 4)
            for a in range(6):
                ins = pe.transpose(PS[0:P, 1024 + a * 128:1024 + (a + 1) * 128], YT[:, a, 0:P], ident[:, :])
            ins.then_inc(S("cbk"), 1)
            pe.wait_ge(S("xn"), 1)
            for n in range((J + 7) // 8):
                if n >= 2:
                    pe.wait_ge(S("t2_ev"), n - 1)
                bank = PS[0:6 * F, (n % 2) * 512:(n % 2 + 1) * 512].bitcast(bf16).rearrange("p (j c) -> p j c", j=8)
                for j in range(8 * n, min(8 * n + 8, J)):
                    ins = pe.transpose(bank[:, j % 8, 0:P], XN[:, j, :], identb[0:P, 0:P])
                ins.then_inc(S("t2"), 1)
            pe.wait_ge(S("l_w6"), 16 * 15)
            pe.wait_ge(S("t2_ev"), (J + 7) // 8)
            for j in range(J):
                for n in range(3):
                    i = 3 * j + n
                    if j >= 2 and n < 2:
                        pe.wait_ge(S("rel_act"), 2 * (j - 2) + n + 1)
                    if j >= 2 and n == 2:
                        pe.wait_ge(S("rel_evd"), j - 1)
                    bank = 1024 + (i % 6) * 512
                    pe.matmul(PS[0:P, bank:bank + 510], NT6[:, j * P:(j + 1) * P], WR6[:, n * 510:(n + 1) * 510],
                              start=True, stop=True).then_inc(S("rel_mm"), 1)
            pe.wait_ge(S("rel_act"), 2 * J)
            pe.wait_ge(S("rel_evd"), J)
            carries("rel", 0)
            node_transposes("t3", "h_nn")
            pe.wait_ge(S("l_w3"), 16 * 10)
            pe.wait_ge(S("t3_ev"), (J + 3) // 4)
            for n in range((J + 2) // 3):
                if n >= 2:
                    pe.wait_ge(S("nn_ev"), n - 1)
                for j in range(3 * n, min(3 * n + 3, J)):
                    at = 1024 + (n % 2) * 512 + (j % 3) * (PW + F)
                    ins = pe.matmul(PS[0:P, at:at + PW + F], nodeT[:, j * P:(j + 1) * P], wk[:, 0:PW + F],
                                    start=True, stop=True)
                ins.then_inc(S("nn_mm"), 1)
            carries("nn", 0)

        @block.vector
        def _(dve):
            v = nc.vector
            count = [0]

            def link(ins):
                count[0] += 1
                ins.then_inc(S("dve"), 1)
                dve.wait_ge(S("dve"), count[0])

            def bc(ap, n):
                return ap.unsqueeze(2).broadcast_to([ap.shape[0], ap.shape[1], n])

            def mid(ap, n):
                return ap.unsqueeze(1).broadcast_to([ap.shape[0], n, ap.shape[1]])

            v.memset(nextd[:, C - 1:C], -1)
            link(v.memset(ones[:, :], 1.0))
            dve.wait_ge(S("pw"), 1)
            v.memset(hv[:, 3:4], float(E)).then_inc(S("cst"), 1)
            dve.wait_ge(S("id"), 2)
            v.tensor_copy(identb[:, :], ident[:, :])
            dve.wait_ge(S("l_dst"), 32)
            v.tensor_copy(subi, dsti.rearrange("p (k w) -> p k w", w=SUBW)[:, :, 0]).then_inc(S("sub"), 1)
            dve.wait_ge(S("iota"), 2)
            link(v.tensor_copy(ncol[:, :], qi[:, :]))
            dve.wait_ge(S("l_nb"), 64)
            link(v.tensor_tensor(keep[:, :], dsti, prevd, ALU.is_equal))
            v.tensor_copy(KR0[:, :, 1], keep[:, :])
            v.tensor_scalar(KR0[:, :, 0], keep[:, :], 1.0, BIG, ALU.subtract, ALU.mult)
            link(v.tensor_reduce(one_run[:, :], keep[:, :], X, ALU.min))
            link(v.tensor_tensor(fend, dsti, nextd, ALU.is_equal))
            link(v.scalar_tensor_tensor(iend, fend, FAR, dsti, ALU.mult, ALU.add))
            dve.wait_ge(S("l_st"), 32)
            v.scalar_tensor_tensor(irel, srci, float(R), typi, ALU.mult, ALU.add).then_inc(S("krs"), 1)
            dve.wait_ge(S("l_bnd"), 16)
            v.tensor_copy(small[0:1, 400:400 + P], small[0:1, 400:400 + P].bitcast(i32)).then_inc(S("bnd"), 1)
            dve.wait_ge(S("bnd_b"), 1)
            w3 = wide.rearrange("p (j q) -> p j q", j=J)
            link(v.tensor_tensor(w3, mid(PS[0:P, 0:P], J), bc(ncol[:, :], P), ALU.is_lt))
            link(v.tensor_reduce(qf[:, :], w3, X, ALU.add))
            link(v.tensor_scalar(qf[:, :], qf[:, :], 1.0, 0.0, ALU.subtract, ALU.max))
            v.tensor_copy(qi[:, :], qf[:, :]).then_inc(S("q1"), 1)
            dve.wait_ge(S("g_sub"), 16 * J)
            g2v = g2.rearrange("p (j q) -> p j q", j=J)
            w2v = wide[:, 0:J * SUB].rearrange("p (j q) -> p j q", j=J)
            link(v.tensor_tensor(w2v, g2v, bc(ncol[:, :], SUB), ALU.is_lt))
            link(v.tensor_reduce(rp[:, :], w2v, X, ALU.add))
            link(v.tensor_scalar(rp[:, :], rp[:, :], 1.0, 0.0, ALU.subtract, ALU.max))
            link(v.scalar_tensor_tensor(qf[:, :], qf[:, :], float(SUB), rp[:, :], ALU.mult, ALU.add))
            v.tensor_copy(si[:, :], qf[:, :]).then_inc(S("q2"), 1)
            dve.wait_ge(S("g_row"), 16 * J)
            g3v = g3.rearrange("p (j q) -> p j q", j=J)
            w4v = wide[:, 0:J * SUBW].rearrange("p (j q) -> p j q", j=J)
            link(v.tensor_tensor(w4v, g3v, bc(ncol[:, :], SUBW), ALU.is_lt))
            link(v.tensor_reduce(st1[:, :], w4v, X, ALU.add))
            v.scalar_tensor_tensor(rp[:, :], qf[:, :], float(SUBW), st1[:, :], ALU.mult, ALU.add).then_inc(S("rp"), 1)
            dve.wait_ge(S("l_rpn"), 16)
            link(v.tensor_scalar(st2[:, :], rpn[:, :], 1.0, 0.0, ALU.subtract, ALU.max))
            v.tensor_copy(endpos[:, :], st2[:, :]).then_inc(S("endpos"), 1)
            dve.wait_ge(S("rp"), 1)
            link(v.tensor_tensor(qf[:, :], rpn[:, :], rp[:, :], ALU.subtract))
            link(v.tensor_scalar(has[:, :], qf[:, :], 0.5, None, ALU.is_gt))
            v.tensor_scalar(st1[:, :], qf[:, :], 1.0, None, ALU.add).then_inc(S("deg_var"), 1)
            dve.wait_ge(S("deg_std"), 1)
            link(v.reciprocal(dinv[:, :], st2[:, :]))

            dve.wait_ge(S("g_head"), 16)
            link(v.tensor_copy(hv[:, 0:1], head_pos[:, :]))
            link(v.tensor_copy(hv[:, 1:2], small[0:P, 600:601].bitcast(i32)))
            link(v.tensor_tensor(hv[:, 1:2], hv[:, 0:1], hv[:, 1:2], ALU.is_lt))
            link(v.tensor_tensor(hv[:, 1:2], hv[:, 1:2], keep[:, 0:1], ALU.mult))
            link(v.tensor_scalar(hv[:, 1:2], hv[:, 1:2], 1.0, -FAR, ALU.subtract, ALU.mult))
            link(v.tensor_tensor(head_row[:, :], hv[:, 1:2], hv[:, 0:1], ALU.add))
            link(v.tensor_tensor(head_node[:, :], hv[:, 1:2], dsti[:, 0:1], ALU.add))

            dve.wait_ge(S("l_w"), 16 * 11)
            v.tensor_copy(carryT[0:F, 0:P], small[0:F, 17:18].broadcast_to([F, P])).then_inc(S("wa2"), 1)
            dve.wait_ge(S("gate_v"), 1)
            gv = small[0:P, 900:900 + F]
            link(v.tensor_copy(gv, PS[0:P, 1024:1024 + F]))
            link(v.tensor_copy(wk[:, :].rearrange("i (r c) -> i r c", c=TW)[:, :, F],
                               PS[0:F, 512:513].broadcast_to([F, R])))
            v.tensor_copy(carryT[0:F, 0:P], small[0:F, 18:19].broadcast_to([F, P])).then_inc(S("wa3"), 1)
            dve.wait_ge(S("gate_v"), 2)
            link(v.tensor_copy(gdst[:, :], PS[0:P, 1536:1536 + F]))
            dve.wait_ge(S("wct"), 1)
            v.tensor_copy(small[0:NB, 480:480 + R], PS[0:NB, 2048:2048 + R]).then_inc(S("wct_c"), 1)
            dve.wait_ge(S("wrel_p"), 1)
            v.tensor_copy(small[0:R, 640:640 + F * F], PS[0:R, 2560:2560 + F * F]).then_inc(S("wrel"), 1)
            v.tensor_scalar(diag[:, :], ident[0:P, 0:P], one_run[:, 0:1], None, ALU.mult).then_inc(S("diag"), 1)
            dve.wait_ge(S("run_p"), 1)
            link(v.tensor_copy(runT[:, :], PS[:, 3072:3072 + P]))
            v.tensor_scalar(resT[:, :], runT[:, :], 1.0, BIG, ALU.subtract, ALU.mult).then_inc(S("setup"), 1)

            def norm(name, done):
                link(v.tensor_reduce(qf[:, :], x[:, :, :], X, ALU.add))
                link(v.tensor_scalar(qf[:, :], qf[:, :], 1.0 / F, None, ALU.mult))
                link(v.tensor_tensor(h[:, :, :], x[:, :, :], bc(qf[:, :], F), ALU.subtract))
                link(v.tensor_tensor(tmp[:, :, :], h[:, :, :], h[:, :, :], ALU.mult))
                link(v.tensor_reduce(st1[:, :], tmp[:, :, :], X, ALU.add))
                v.tensor_scalar(st1[:, :], st1[:, :], 1.0 / F, EPS, ALU.mult, ALU.add).then_inc(S(f"{name}_var"), 1)
                dve.wait_ge(S(f"{name}_var"), 1)
                dve.wait_ge(S(f"{name}_std"), 1)
                link(v.reciprocal(st2[:, :], st2[:, :]))
                link(v.tensor_tensor(h[:, :, :], h[:, :, :], bc(st2[:, :], F), ALU.mult))
                ins = v.tensor_scalar(h[:, :, :], h[:, :, :], 0.0, None, ALU.max)
                if done:
                    ins.then_inc(S(done), 1)
                    dve.wait_ge(S(done), 1)
                else:
                    link(ins)

            def narrow(L):
                W, w = GROW[L], WIDTH[L]
                g = G[:, 0:2 * BL * W].rearrange("p (s t c) -> p s t c", s=2, t=BL)
                r = SR[:, 0:2 * BL * w].rearrange("p (s t c) -> p s t c", s=2, t=BL)
                m = V[:, 0:BL * F].rearrange("p (t c) -> p t c", t=BL)
                sc = V[:, BL * F:BL * F + BL]
                own = S(f"{L}_dve")

                def step(b, s, k, first):
                    dve.wait_ge(S(f"n_g{s}"), upto(L, f"g{s}", 16 * BL * (k + 1)))
                    if not first or b > 0:
                        dve.wait_ge(S("n_run"), upto(L, "run", b))
                    if not first:
                        dve.wait_ge(S(f"n_r{s}"), upto(L, f"r{s}", 16 * k))
                    if L == "rel":
                        v.tensor_tensor(sc, g[:, s, :, F], gate_e[:, bass.ds(b * BL, BL)], ALU.add).then_inc(own, 1)
                        dve.wait_ge(own, 2 * b + 1)
                        v.tensor_tensor(m, g[:, s, :, 0:F], bc(sc, F), ALU.mult).then_inc(own, 1)
                        dve.wait_ge(own, 2 * b + 2)
                    if L == "nn":
                        tm = TM.rearrange("p (t c k) -> p t c k", t=BL, k=D8)
                        dve.wait_ge(S(f"ea8_{s}"), 16 * (k + 1))
                        e8 = EA[:, s * BL * D8:(s + 1) * BL * D8].rearrange("p (t k) -> p t k", k=D8)
                        v.tensor_tensor(tm, g[:, s, :, 0:F * D8].rearrange("p t (c k) -> p t c k", k=D8),
                                        e8.unsqueeze(2).broadcast_to([P, BL, F, D8]), ALU.mult).then_inc(own, 1)
                        dve.wait_ge(own, 3 * b + 1)
                        v.tensor_reduce(m, tm, X, ALU.add).then_inc(own, 1)
                        dve.wait_ge(own, 3 * b + 2)
                        v.tensor_tensor(m, m, g[:, s, :, F * D8:PW], ALU.add).then_inc(own, 1)
                        dve.wait_ge(own, 3 * b + 3)
                    kb = keep[:, bass.ds(b * BL, BL)]
                    for f in range(w):
                        if L == "rel":
                            data = m[:, :, f] if f < F else g[:, s, :, f - F]
                        else:
                            data = m[:, :, f] if L == "nn" else g[:, s, :, f]
                        zero_start = first and s == 0
                        ins = v.tensor_tensor_scan(r[:, s, :, f], kb, data,
                                                   0.0 if zero_start else r[:, 1 - s, BL - 1:BL, f], ALU.mult, ALU.add)
                    ins.then_inc(S("n_run"), 1)
                    dve.wait_ge(S("n_run"), upto(L, "run", b + 1))
                    if L == "conv1":
                        dve.wait_ge(S(f"ea16_{s}"), 16 * (k + 1))
                        if not first or b > 0:
                            dve.wait_ge(S("x6_tr"), 5 * b)
                        a = EA[:, s * BL * F:(s + 1) * BL * F].rearrange("p (t f) -> p t f", f=F)
                        n = [0]

                        def own_link(i):
                            n[0] += 1
                            i.then_inc(own, 1)
                            dve.wait_ge(own, 8 * b + n[0])

                        own_link(v.tensor_copy(X6[:, :, 0:F], a))
                        v.tensor_copy(X6[:, :, F:3 * F].rearrange("p t (a f) -> p t a f", a=2),
                                      X6[:, :, 0:F].unsqueeze(2).broadcast_to([P, BL, 2, F]))
                        own_link(v.tensor_tensor(r1, a, X6[:, :, 0:F], ALU.subtract))
                        own_link(v.tensor_copy(X6[:, :, 3 * F:4 * F], r1))
                        own_link(v.tensor_copy(X6[:, :, 4 * F:5 * F], X6[:, :, 3 * F:4 * F]))
                        own_link(v.tensor_tensor(r2, r1, X6[:, :, 3 * F:4 * F], ALU.subtract))
                        own_link(v.tensor_copy(X6[:, :, 5 * F:6 * F], r2))
                        own_link(v.memset(X6[:, :, 6 * F:6 * F + 4], 1.0))
                        own_link(v.tensor_tensor(r1, a, mid(gv, BL), ALU.mult))
                        v.tensor_reduce(gate_e[:, bass.ds(b * BL, BL)], r1, X, ALU.add).then_inc(S("split"), 1)
                        dve.wait_ge(S("split"), b + 1)

                blocks(step, HALF, dve.Fori)
                link(v.memset(carryT[:, 0:1], 0.0))
                dve.wait_ge(S("n_tt"), upto(L, "tt", 1))
                link(v.tensor_copy(small[0:w, 920:920 + P], PS[0:w, 3072:3072 + P]))
                v.tensor_tensor_scan(carryT[0:w, 1:P + 1], runT[0:w, :], small[0:w, 920:920 + P], 0.0,
                                     ALU.mult, ALU.add).then_inc(S("n_cs"), 1)
                dve.wait_ge(S("n_cb"), upto(L, "cb", 1))
                dve.wait_ge(S("n_hg"), upto(L, "hg", 16))
                v.tensor_tensor(headb[:, 0:w], headb[:, 0:w], PS[0:P, 3584:3584 + w], ALU.add).then_inc(S("n_merged"), 1)
                dve.wait_ge(S("n_ns"), upto(L, "ns", 16 * J))
                ns = NS[:, 0:J * w].rearrange("p (j c) -> p j c", j=J)
                link(v.tensor_tensor(ns, ns, bc(has[:, :], w), ALU.mult))
                return ns

            dve.wait_ge(S("l_x"), 16)
            norm("ln1", None)
            v.tensor_tensor(h[:, :, :], h[:, :, :], bc(dinv[:, :], F), ALU.mult).then_inc(S("h_conv1"), 1)
            dve.wait_ge(S("h_conv1"), 1)
            dve.wait_ge(S("d_idx"), 96)
            ns = narrow("conv1")
            link(v.tensor_tensor(h[:, :, :], ns, h[:, :, :], ALU.add))
            v.tensor_tensor(h[:, :, :], h[:, :, :], bc(dinv[:, :], F), ALU.mult).then_inc(S("agg1"), 1)
            dve.wait_ge(S("conv2_in"), 1)
            for a, b in ((0, 32), (32, J)):
                ins = v.tensor_tensor(h[:, a:b, :], PS[0:P, 2048 + a * F:2048 + b * F].rearrange("p (j f) -> p j f", f=F),
                                      bc(dinv[:, a:b], F), ALU.mult)
            ins.then_inc(S("h_conv2"), 1)
            dve.wait_ge(S("h_conv2"), 1)
            ns = narrow("conv2")
            link(v.tensor_tensor(h[:, :, :], ns, h[:, :, :], ALU.add))
            link(v.tensor_tensor(h[:, :, :], h[:, :, :], bc(dinv[:, :], F), ALU.mult))
            link(v.tensor_tensor(h[:, :, :], h[:, :, :], mid(bias[:, 0, :], J), ALU.add))
            link(v.tensor_tensor(x[:, :, :], x[:, :, :], h[:, :, :], ALU.add))
            norm("ln2", "h_soft")

            dve.wait_ge(S("d_zero"), 320)
            dve.wait_ge(S("l_w1"), 64)
            for n in range(3):
                v.tensor_copy(W1B[:, n, :], W1F).then_inc(S("w1_parts"), 1)
                dve.wait_ge(S("w1_parts"), n + 1)
                if n < 2:
                    link(v.tensor_tensor(W1F, W1F, W1B[:, n, :], ALU.subtract))
            v.tensor_scalar(neg, ident[0:P, 0:P], -1.0, None, ALU.mult).then_inc(S("neg"), 1)
            link(v.memset(XS[:, 2, B1 - 1, 0:CH], -BIG))
            link(v.memset(XS[:, 2, B1 - 1, CH:ROW], 0.0))

            def maxima(b, s):
                for n in range(MAXES):
                    if n == 0:
                        dve.wait_ge(S("soft_prod"), 4 * b + 4)
                    else:
                        dve.wait_ge(S("soft_max"), MAXES * b + n)
                    if n < B1:
                        prev = XS[:, s, n - 1, 0:CH] if n else XS[:, (s + 2) % 3, B1 - 1, 0:CH]
                        v.scalar_tensor_tensor(XS[:, s, n, 0:CH], prev, KR[:, s, n, 0:1], XS[:, s, n, CH:2 * CH],
                                               ALU.add, ALU.max).then_inc(S("soft_max"), 1)
                    else:
                        t = MAXES - 1 - n
                        v.scalar_tensor_tensor(XS[:, s, t, 0:CH], XS[:, s, t + 1, 0:CH], KR[:, s, t + 1, 0:1],
                                               XS[:, s, t, 0:CH], ALU.add, ALU.max).then_inc(S("soft_max"), 1)
                    yield

            def sums(b, s):
                dve.wait_ge(S("soft_exp"), 6 * b + 6)
                for t in range(0, B1, 2):
                    v.tensor_tensor(XS[:, s, t:t + 2, 2 * CH:ROW], XS[:, s, t:t + 2, 2 * CH:ROW],
                                    XS[:, s, t:t + 2, CH:2 * CH], ALU.mult).then_inc(S("soft_num"), 1)
                    yield
                dve.wait_ge(S("soft_done"), b) if not isinstance(b, int) or b > 0 else None
                v.tensor_tensor(SC, XS[:, (s + 2) % 3, B1 - 1, CH:ROW].rearrange("p (a c) -> p a c", a=2), mid(DC, 2),
                                ALU.mult).then_inc(S("soft_carry"), 1)
                yield
                for t in range(B1):
                    to = XS[:, s, t, CH:ROW]
                    if t == 0:
                        dve.wait_ge(S("soft_num"), 5 * b + 5)
                        dve.wait_ge(S("soft_carry"), b + 1)
                        ins = v.tensor_tensor(to, to, SC.rearrange("p a c -> p (a c)"), ALU.add)
                    else:
                        dve.wait_ge(S("soft_sum"), (B1 - 1) * b + t)
                        ins = v.scalar_tensor_tensor(to, XS[:, s, t - 1, CH:ROW], KR[:, s, t, 1:2], to, ALU.mult, ALU.add)
                    ins.then_inc(S("soft_sum") if t < B1 - 1 else S("soft_done"), 1)
                    yield

            def soft(b, s, k, first):
                dve.wait_ge(S(f"soft_g{s}"), 16 * B1 * (k + 1))
                dve.wait_ge(S(f"soft_k{s}"), 32 * (k + 1))
                if not first:
                    dve.wait_ge(S(f"soft_s{s}"), 16 * B1 * k)
                t = 0
                for g, n in enumerate(GROUPS):
                    dve.wait_ge(S("soft_mm"), 4 * b + g + 1)
                    at = 3 * (g % 2) * 512
                    for a in range(2):
                        ins = v.tensor_tensor(XS[:, s, t:t + n, (1 + a) * CH:(2 + a) * CH].rearrange("p t (i o) -> p t i o", i=F),
                                              PS[0:P, at:at + n * 512].rearrange("p (t a i o) -> p t a i o", a=2, i=F, o=F)[:, :, a],
                                              GH[:, s, t:t + n, :].unsqueeze(3).broadcast_to([P, n, F, F]), ALU.mult)
                    ins.then_inc(S("soft_prod"), 1)
                    t += n
                other = iter(()) if first and s == 0 else sums(b - 1, (s + 2) % 3)
                for _ in maxima(b, s):
                    next(other, None)
                for _ in other:
                    pass

            triples(soft, dve.Fori)
            for _ in sums(NB1 - 1, 2):
                pass
            dve.wait_ge(S("ct"), 1)
            v.tensor_copy(CT[:, 0:4, :], PS[:, 0:512].rearrange("p (a c) -> p a c", a=4)[:, :, 0:P])
            link(v.tensor_copy(CT[:, 4:6, :], PS[:, 512:768].rearrange("p (a c) -> p a c", a=2)[:, :, 0:P]))
            v.memset(YT[:, 0:2, 0:1], -BIG)
            link(v.memset(YT[:, 2:6, 0:1], 0.0))
            for a in range(2):
                link(v.tensor_tensor_scan(YT[:, a, 1:P + 1], resT[:, :], CT[:, a, :], -BIG, ALU.add, ALU.max))
                link(v.tensor_tensor(FT[:, a, :], YT[:, a, 0:P], resT[:, :], ALU.add))
                link(v.tensor_tensor(FT[:, a, :], FT[:, a, :], YT[:, a, 1:P + 1], ALU.subtract))
                v.tensor_tensor(FT[:, 2 + a, :], CT[:, a, :], YT[:, a, 1:P + 1], ALU.subtract).then_inc(S("cd"), 1)
            dve.wait_ge(S("ce"), 1)
            for a in range(2):
                for n in (2, 4):
                    link(v.tensor_tensor(CT[:, n + a, :], CT[:, n + a, :], FT[:, 2 + a, :], ALU.mult))
                    v.tensor_tensor_scan(YT[:, n + a, 1:P + 1], FT[:, a, :], CT[:, n + a, :], 0.0, ALU.mult, ALU.add).then_inc(S("cc"), 1)
            dve.wait_ge(S("cbk"), 1)
            link(v.tensor_copy(CB, PS[0:P, 1024:1024 + ROW]))
            dve.wait_ge(S("soft_hg"), 16)
            link(v.tensor_tensor(HM[:, 2, :], HG[:, 0:CH], CB[:, 0:CH], ALU.max))
            v.tensor_tensor(HM[:, 0, :], HG[:, 0:CH], HM[:, 2, :], ALU.subtract)
            v.tensor_tensor(HM[:, 1, :], CB[:, 0:CH], HM[:, 2, :], ALU.subtract).then_inc(S("hd"), 1)
            dve.wait_ge(S("he"), 1)
            for part, m in ((HG, 0), (CB, 1)):
                two = part[:, CH:ROW].rearrange("p (a c) -> p a c", a=2)
                link(v.tensor_tensor(two, two, mid(HM[:, m, :], 2), ALU.mult))
            link(v.tensor_tensor(HG[:, CH:ROW], HG[:, CH:ROW], CB[:, CH:ROW], ALU.add))
            v.tensor_copy(HG[:, 0:CH], HM[:, 2, :]).then_inc(S("soft_merged"), 1)
            dve.wait_ge(S("l_wk"), 16)
            for n in range(3):
                v.tensor_copy(WRB[:, n, :], wk[:, :]).then_inc(S("wk_parts"), 1)
                dve.wait_ge(S("wk_parts"), n + 1)
                if n < 2:
                    link(v.tensor_tensor(wk[:, :], wk[:, :], WRB[:, n, :], ALU.subtract))
            for n in range(J // 5):
                dve.wait_ge(S(f"soft_l{n % 2}"), 32 * (n // 2 + 1))
                rows = NODE[:, n % 2]
                link(v.tensor_scalar(rows[:, :, 0:CH], rows[:, :, CH:2 * CH], 1e-30, None, ALU.max))
                link(v.reciprocal(rows[:, :, 0:CH], rows[:, :, 0:CH]))
                link(v.tensor_tensor(rows[:, :, 0:CH], rows[:, :, 0:CH], rows[:, :, 2 * CH:ROW], ALU.mult))
                v.tensor_reduce(tmp[:, 5 * n:5 * n + 5, :], rows[:, :, 0:CH].rearrange("p j (i o) -> p j o i", i=F),
                                X, ALU.add).then_inc(S("soft_n"), 1)
                dve.wait_ge(S("soft_n"), n + 1)
            link(v.tensor_tensor(x[:, :, :], x[:, :, :], tmp[:, :, :], ALU.add))
            norm("ln3", None)

            link(v.tensor_copy(XN[:, :, 0:F], h[:, :, :]))
            link(v.tensor_copy(XN[:, :, F:3 * F].rearrange("p t (a f) -> p t a f", a=2),
                               XN[:, :, 0:F].unsqueeze(2).broadcast_to([P, J, 2, F])))
            link(v.tensor_tensor(tmp[:, :, :], h[:, :, :], XN[:, :, 0:F], ALU.subtract))
            link(v.tensor_copy(XN[:, :, 3 * F:4 * F], tmp[:, :, :]))
            link(v.tensor_copy(XN[:, :, 4 * F:5 * F], XN[:, :, 3 * F:4 * F]))
            link(v.tensor_tensor(tmp2[:, :, :], tmp[:, :, :], XN[:, :, 3 * F:4 * F], ALU.subtract))
            v.tensor_copy(XN[:, :, 5 * F:6 * F], tmp2[:, :, :]).then_inc(S("xn"), 1)
            link(v.tensor_tensor(tmp[:, :, :], h[:, :, :], mid(gdst[:, :], J), ALU.mult))
            link(v.tensor_reduce(qf[:, :], tmp[:, :, :], X, ALU.add))
            for j in range(J):
                dve.wait_ge(S("rel_mm"), 3 * j + 3)
                if j >= 4:
                    dve.wait_ge(S(f"rel_t{j % 4}"), 32 * (j // 4))
                bank = 1024 + ((3 * j + 2) % 6) * 512
                v.tensor_copy(TR[:, j % 4, 1020:1530], PS[0:P, bank:bank + 510]).then_inc(S("rel_evd"), 1)
            for s in range(4):
                dve.wait_ge(S(f"rel_t{s}"), 32 * ((J - s + 3) // 4))
            ns = narrow("rel")
            link(v.tensor_tensor(tmp[:, :, :], ns[:, :, F:2 * F], bc(qf[:, :], F), ALU.mult))
            link(v.tensor_tensor(tmp[:, :, :], tmp[:, :, :], ns[:, :, 0:F], ALU.add))
            v.tensor_tensor(x[:, :, :], x[:, :, :], tmp[:, :, :], ALU.add).then_inc(S("rel_nodes"), 1)
            dve.wait_ge(S("rel_nodes"), 1)
            norm("ln4", "h_nn")

            dve.wait_ge(S("nn_rows"), 1)
            link(v.tensor_tensor(x[:, :, :], x[:, :, :], tmp2[:, :, :], ALU.add))
            link(v.tensor_tensor(x[:, :, :], x[:, :, :], mid(bias[:, 1, :], J), ALU.add))
            dve.wait_ge(S("tab_nn"), 16)
            ns = narrow("nn")
            v.tensor_tensor(x[:, :, :], x[:, :, :], ns, ALU.add).then_inc(S("x_out"), 1)


_OUTS = [((N, F), 'float32')]


def kernel(**inputs):
    import numpy as _np
    import concourse.bacc as _bacc
    from concourse import mybir as _mybir
    from concourse.bass_utils import run_bass_kernel_spmd as _run

    nc = _bacc.Bacc("TRN2", target_bir_lowering=False, num_devices=1)
    arrays, args = {}, {}
    for name in sorted(inputs):
        a = _np.ascontiguousarray(inputs[name])
        arrays[f"in_{name}"] = a
        args[name] = nc.dram_tensor(f"in_{name}", a.shape, _mybir.dt.from_np(a.dtype), kind="ExternalInput").ap()
    out = nc.dram_tensor("out_0", _OUTS[0][0], _mybir.dt.float32, kind="ExternalOutput").ap()
    graph_layers(nc, args, out)
    r = _run(nc, [arrays], core_ids=[0])
    return r.results[0]["out_0"]
```
